# Optimizing a Trainium2 kernel written in Bass

```python
import numpy as np
import jax
import jax.numpy as jnp

def _softmax(x, axis=-1):
    return jax.nn.softmax(x, axis=axis)

def _gelu(x):
    return jax.nn.gelu(x, approximate=True)

def _silu(x):
    return jax.nn.silu(x)

def _sigmoid(x):
    return jax.nn.sigmoid(x)

def _layernorm(x, axis=-1, eps=1e-05):
    m = jnp.mean(x, axis=axis, keepdims=True)
    v = jnp.var(x, axis=axis, keepdims=True)
    return (x - m) / jnp.sqrt(v + eps)

def _scatter_add(tgt, idx, src, axis=0):
    return tgt.at[idx].add(src)

def _segment_sum(src, seg, n):
    return jax.ops.segment_sum(src, seg, n)
kernel_name = 'mk_vit_tower_d1_tok_img768_r4_ecd18a'

def setup_inputs(seed: int=0):
    np.random.seed(seed)
    _w = jnp.asarray

    def _rec_inputs():
        import jax
        import jax.numpy as jnp
        _rk = jax.random.key(seed)
        x = -7.10856e-05 + 0.999911 * jax.random.normal(jax.random.fold_in(_rk, 1), (2, 32, 128, 128), jnp.float32)
        return x
    x = _rec_inputs()

    def _L0_tok_setup():
        import jax, jax.numpy as jnp
        import numpy as np
        B, C, H, W = (8, 32, 128, 128)
        P = 8
        D = 128
        NH, DH = (8, 64)
        M = 512
        L = 2
        DOUT = 192
        INNER = NH * DH

        def _ln(x, g, b, eps=1e-05):
            mu = x.mean(-1, keepdims=True)
            xc = x - mu
            var = (xc * xc).mean(-1, keepdims=True)
            return xc * jax.lax.rsqrt(var + eps) * g + b

        def _forward(im, conv_w, conv_b, ln1_g, ln1_b, qkv_w, out_w, out_b, ln2_g, ln2_b, ff1_w, ff1_b, ff2_w, ff2_b, lnf_g, lnf_b, head_w, head_b):
            b, c, h, w = im.shape
            hp, wp = (h // P, w // P)
            patches = im.reshape(b, c, hp, P, wp, P)
            x = jnp.einsum('bchpwq,dcpq->bhwd', patches, conv_w)
            x = x.reshape(b, hp * wp, -1) + conv_b
            n = hp * wp
            scale = DH ** (-0.5)
            for i in range(ln1_g.shape[0]):
                y = _ln(x, ln1_g[i], ln1_b[i])
                qkv = y @ qkv_w[i]
                q, k, v = jnp.split(qkv, 3, axis=-1)
                to_heads = lambda t: t.reshape(b, n, NH, DH).transpose(0, 2, 1, 3)
                q, k, v = (to_heads(q), to_heads(k), to_heads(v))
                q = jax.nn.softmax(q, axis=-1) * scale
                k = jax.nn.softmax(k, axis=-2)
                ctx = jnp.einsum('bhnd,bhne->bhde', k, v)
                att = jnp.einsum('bhnd,bhde->bhne', q, ctx)
                att = att.transpose(0, 2, 1, 3).reshape(b, n, INNER)
                x = x + att @ out_w[i] + out_b[i]
                y = _ln(x, ln2_g[i], ln2_b[i])
                hdn = jax.nn.gelu(y @ ff1_w[i] + ff1_b[i], approximate=False)
                x = x + hdn @ ff2_w[i] + ff2_b[i]
            return _ln(x, lnf_g, lnf_b) @ head_w + head_b
        key = jax.random.key(seed)
        ks = iter(jax.random.split(key, 32))
        g = lambda shape, s=0.02: (jax.random.normal(next(ks), shape) * s).astype(jnp.float32)
        inp = {'im': jax.random.normal(next(ks), (B, C, H, W), dtype=jnp.float32), 'conv_w': g((D, C, P, P)), 'conv_b': jnp.zeros((D,), jnp.float32), 'ln1_g': jnp.ones((L, D), jnp.float32), 'ln1_b': jnp.zeros((L, D), jnp.float32), 'qkv_w': g((L, D, 3 * INNER)), 'out_w': g((L, INNER, D)), 'out_b': jnp.zeros((L, D), jnp.float32), 'ln2_g': jnp.ones((L, D), jnp.float32), 'ln2_b': jnp.zeros((L, D), jnp.float32), 'ff1_w': g((L, D, M)), 'ff1_b': jnp.zeros((L, M), jnp.float32), 'ff2_w': g((L, M, D)), 'ff2_b': jnp.zeros((L, D), jnp.float32), 'lnf_g': jnp.ones((D,), jnp.float32), 'lnf_b': jnp.zeros((D,), jnp.float32), 'head_w': g((D, DOUT)), 'head_b': jnp.zeros((DOUT,), jnp.float32)}
        return inp
    _L0_tok_all = _L0_tok_setup()
    _L0_tok_in = {k: v for k, v in _L0_tok_all.items() if k in ('conv_w', 'conv_b', 'ln1_g', 'ln1_b', 'qkv_w', 'out_w', 'out_b', 'ln2_g', 'ln2_b', 'ff1_w', 'ff1_b', 'ff2_w', 'ff2_b', 'lnf_g', 'lnf_b', 'head_w', 'head_b')}
    del _L0_tok_all

    def _L0_attn_setup():
        import jax, jax.numpy as jnp
        import numpy as np
        EPS = 1e-06
        H = 12

        def _phi(x):
            return jax.nn.elu(x) + 1.0
        key = jax.random.key(seed)
        k1, k2, k3 = jax.random.split(key, 3)
        B, N, D = (32, 256, 192)
        x = jax.random.normal(k1, (B, N, D), dtype=jnp.float32)
        W_qkv = jax.random.normal(k2, (D, 3 * D), dtype=jnp.float32) * D ** (-0.5)
        W_out = jax.random.normal(k3, (D, D), dtype=jnp.float32) * D ** (-0.5)
        b_out = jnp.zeros((D,), dtype=jnp.float32)
        return {'x': x, 'W_qkv': W_qkv, 'W_out': W_out, 'b_out': b_out}
    _L0_attn_all = _L0_attn_setup()
    _L0_attn_in = {k: v for k, v in _L0_attn_all.items() if k in ('W_qkv', 'W_out', 'b_out')}
    del _L0_attn_all

    def _L0_ffn_setup():
        import math
        import jax, jax.numpy as jnp
        import numpy as np
        EMBED_CHOICES = [96, 144, 192]
        RATIO_CHOICES = [2, 3, 4]
        E_MAX = 192
        H_MAX = 768

        def new_gelu(x):
            c = math.sqrt(2.0 / math.pi)
            return 0.5 * x * (1.0 + jnp.tanh(c * (x + 0.044715 * x * x * x)))

        def _mixed_coeffs(alpha_e, alpha_r):
            h_idx = jnp.arange(H_MAX)
            d_idx = jnp.arange(E_MAX)
            C0 = jnp.zeros((H_MAX, E_MAX), jnp.float32)
            c0b = jnp.zeros((H_MAX,), jnp.float32)
            C1 = jnp.zeros((E_MAX, H_MAX), jnp.float32)
            c1b = jnp.zeros((E_MAX,), jnp.float32)
            for i, e in enumerate(EMBED_CHOICES):
                m_in = (d_idx < e).astype(jnp.float32)
                for j, r in enumerate(RATIO_CHOICES):
                    a = alpha_e[i] * alpha_r[j]
                    m_out = (h_idx < r * e).astype(jnp.float32)
                    C0 = C0 + a * (m_out[:, None] * m_in[None, :])
                    c0b = c0b + a * m_out
                    C1 = C1 + a * (m_in[:, None] * m_out[None, :])
                    c1b = c1b + a * m_in
            return (C0, c0b, C1, c1b)
        key = jax.random.key(seed)
        ks = jax.random.split(key, 6)
        x = jax.random.normal(ks[0], (8, 512, E_MAX), jnp.float32)
        w_fc = jax.random.normal(ks[1], (H_MAX, E_MAX), jnp.float32) * 0.02
        b_fc = jnp.zeros((H_MAX,), jnp.float32)
        w_proj = jax.random.normal(ks[2], (E_MAX, H_MAX), jnp.float32) * 0.02
        b_proj = jnp.zeros((E_MAX,), jnp.float32)
        alpha_e = jax.nn.softmax(jax.random.normal(ks[3], (3,), jnp.float32))
        alpha_r = jax.nn.softmax(jax.random.normal(ks[4], (3,), jnp.float32))
        return {'x': x, 'w_fc': w_fc, 'b_fc': b_fc, 'w_proj': w_proj, 'b_proj': b_proj, 'alpha_e': alpha_e, 'alpha_r': alpha_r}
    _L0_ffn_all = _L0_ffn_setup()
    _L0_ffn_in = {k: v for k, v in _L0_ffn_all.items() if k in ('w_fc', 'b_fc', 'w_proj', 'b_proj', 'alpha_e', 'alpha_r')}
    del _L0_ffn_all
    return {'x': x, 'L0_tok_conv_w': _L0_tok_in['conv_w'], 'L0_tok_conv_b': _L0_tok_in['conv_b'], 'L0_tok_ln1_g': _L0_tok_in['ln1_g'], 'L0_tok_ln1_b': _L0_tok_in['ln1_b'], 'L0_tok_qkv_w': _L0_tok_in['qkv_w'], 'L0_tok_out_w': _L0_tok_in['out_w'], 'L0_tok_out_b': _L0_tok_in['out_b'], 'L0_tok_ln2_g': _L0_tok_in['ln2_g'], 'L0_tok_ln2_b': _L0_tok_in['ln2_b'], 'L0_tok_ff1_w': _L0_tok_in['ff1_w'], 'L0_tok_ff1_b': _L0_tok_in['ff1_b'], 'L0_tok_ff2_w': _L0_tok_in['ff2_w'], 'L0_tok_ff2_b': _L0_tok_in['ff2_b'], 'L0_tok_lnf_g': _L0_tok_in['lnf_g'], 'L0_tok_lnf_b': _L0_tok_in['lnf_b'], 'L0_tok_head_w': _L0_tok_in['head_w'], 'L0_tok_head_b': _L0_tok_in['head_b'], 'L0_attn_W_qkv': _L0_attn_in['W_qkv'], 'L0_attn_W_out': _L0_attn_in['W_out'], 'L0_attn_b_out': _L0_attn_in['b_out'], 'L0_ffn_w_fc': _L0_ffn_in['w_fc'], 'L0_ffn_b_fc': _L0_ffn_in['b_fc'], 'L0_ffn_w_proj': _L0_ffn_in['w_proj'], 'L0_ffn_b_proj': _L0_ffn_in['b_proj'], 'L0_ffn_alpha_e': _L0_ffn_in['alpha_e'], 'L0_ffn_alpha_r': _L0_ffn_in['alpha_r']}

def reference(x, L0_tok_conv_w, L0_tok_conv_b, L0_tok_ln1_g, L0_tok_ln1_b, L0_tok_qkv_w, L0_tok_out_w, L0_tok_out_b, L0_tok_ln2_g, L0_tok_ln2_b, L0_tok_ff1_w, L0_tok_ff1_b, L0_tok_ff2_w, L0_tok_ff2_b, L0_tok_lnf_g, L0_tok_lnf_b, L0_tok_head_w, L0_tok_head_b, L0_attn_W_qkv, L0_attn_W_out, L0_attn_b_out, L0_ffn_w_fc, L0_ffn_b_fc, L0_ffn_w_proj, L0_ffn_b_proj, L0_ffn_alpha_e, L0_ffn_alpha_r):
    import jax
    import jax.numpy as jnp

    def _L0_tok_ref(im, conv_w, conv_b, ln1_g, ln1_b, qkv_w, out_w, out_b, ln2_g, ln2_b, ff1_w, ff1_b, ff2_w, ff2_b, lnf_g, lnf_b, head_w, head_b):
        import jax, jax.numpy as jnp
        import numpy as np
        B, C, H, W = (8, 32, 128, 128)
        P = 8
        D = 128
        NH, DH = (8, 64)
        M = 512
        L = 2
        DOUT = 192
        INNER = NH * DH

        def _ln(x, g, b, eps=1e-05):
            mu = x.mean(-1, keepdims=True)
            xc = x - mu
            var = (xc * xc).mean(-1, keepdims=True)
            return xc * jax.lax.rsqrt(var + eps) * g + b

        def _forward(im, conv_w, conv_b, ln1_g, ln1_b, qkv_w, out_w, out_b, ln2_g, ln2_b, ff1_w, ff1_b, ff2_w, ff2_b, lnf_g, lnf_b, head_w, head_b):
            b, c, h, w = im.shape
            hp, wp = (h // P, w // P)
            patches = im.reshape(b, c, hp, P, wp, P)
            x = jnp.einsum('bchpwq,dcpq->bhwd', patches, conv_w)
            x = x.reshape(b, hp * wp, -1) + conv_b
            n = hp * wp
            scale = DH ** (-0.5)
            for i in range(ln1_g.shape[0]):
                y = _ln(x, ln1_g[i], ln1_b[i])
                qkv = y @ qkv_w[i]
                q, k, v = jnp.split(qkv, 3, axis=-1)
                to_heads = lambda t: t.reshape(b, n, NH, DH).transpose(0, 2, 1, 3)
                q, k, v = (to_heads(q), to_heads(k), to_heads(v))
                q = jax.nn.softmax(q, axis=-1) * scale
                k = jax.nn.softmax(k, axis=-2)
                ctx = jnp.einsum('bhnd,bhne->bhde', k, v)
                att = jnp.einsum('bhnd,bhde->bhne', q, ctx)
                att = att.transpose(0, 2, 1, 3).reshape(b, n, INNER)
                x = x + att @ out_w[i] + out_b[i]
                y = _ln(x, ln2_g[i], ln2_b[i])
                hdn = jax.nn.gelu(y @ ff1_w[i] + ff1_b[i], approximate=False)
                x = x + hdn @ ff2_w[i] + ff2_b[i]
            return _ln(x, lnf_g, lnf_b) @ head_w + head_b
        return _forward(im, conv_w, conv_b, ln1_g, ln1_b, qkv_w, out_w, out_b, ln2_g, ln2_b, ff1_w, ff1_b, ff2_w, ff2_b, lnf_g, lnf_b, head_w, head_b)

    def _L0_attn_ref(x, W_qkv, W_out, b_out):
        import jax, jax.numpy as jnp
        import numpy as np
        EPS = 1e-06
        H = 12

        def _phi(x):
            return jax.nn.elu(x) + 1.0
        B, N, D = x.shape
        d = D // H
        x_ = jnp.pad(x, ((0, 0), (0, 1), (0, 0)))
        qkv = x_ @ W_qkv
        q, k, v = jnp.split(qkv, 3, axis=-1)
        q = q.reshape(B, N + 1, H, d)
        k = k.reshape(B, N + 1, H, d)
        v = v.reshape(B, N + 1, H, d)
        q = _phi(q)
        k = _phi(k)
        kv = jnp.einsum('bshd,bshm->bhdm', k, v)
        z = 1.0 / (jnp.einsum('blhd,bhd->blh', q, k.sum(axis=1)) + EPS)
        out = jnp.einsum('blhd,bhdm,blh->blhm', q, kv, z)
        out = out.reshape(B, N + 1, D)
        out = out @ W_out + b_out
        return out[:, :-1, :]

    def _L0_ffn_ref(x, w_fc, b_fc, w_proj, b_proj, alpha_e, alpha_r):
        import math
        import jax, jax.numpy as jnp
        import numpy as np
        EMBED_CHOICES = [96, 144, 192]
        RATIO_CHOICES = [2, 3, 4]
        E_MAX = 192
        H_MAX = 768

        def new_gelu(x):
            c = math.sqrt(2.0 / math.pi)
            return 0.5 * x * (1.0 + jnp.tanh(c * (x + 0.044715 * x * x * x)))

        def _mixed_coeffs(alpha_e, alpha_r):
            h_idx = jnp.arange(H_MAX)
            d_idx = jnp.arange(E_MAX)
            C0 = jnp.zeros((H_MAX, E_MAX), jnp.float32)
            c0b = jnp.zeros((H_MAX,), jnp.float32)
            C1 = jnp.zeros((E_MAX, H_MAX), jnp.float32)
            c1b = jnp.zeros((E_MAX,), jnp.float32)
            for i, e in enumerate(EMBED_CHOICES):
                m_in = (d_idx < e).astype(jnp.float32)
                for j, r in enumerate(RATIO_CHOICES):
                    a = alpha_e[i] * alpha_r[j]
                    m_out = (h_idx < r * e).astype(jnp.float32)
                    C0 = C0 + a * (m_out[:, None] * m_in[None, :])
                    c0b = c0b + a * m_out
                    C1 = C1 + a * (m_in[:, None] * m_out[None, :])
                    c1b = c1b + a * m_in
            return (C0, c0b, C1, c1b)
        C0, c0b, C1, c1b = _mixed_coeffs(alpha_e, alpha_r)
        W0 = w_fc * C0
        b0 = b_fc * c0b
        h = jnp.einsum('bte,he->bth', x, W0) + b0
        h = new_gelu(h)
        W1 = w_proj * C1
        b1 = b_proj * c1b
        out = jnp.einsum('bth,eh->bte', h, W1) + b1
        return out
    h = _L0_tok_ref(x, L0_tok_conv_w, L0_tok_conv_b, L0_tok_ln1_g, L0_tok_ln1_b, L0_tok_qkv_w, L0_tok_out_w, L0_tok_out_b, L0_tok_ln2_g, L0_tok_ln2_b, L0_tok_ff1_w, L0_tok_ff1_b, L0_tok_ff2_w, L0_tok_ff2_b, L0_tok_lnf_g, L0_tok_lnf_b, L0_tok_head_w, L0_tok_head_b)
    h = h + _L0_attn_ref(_layernorm(h, axis=-1), L0_attn_W_qkv, L0_attn_W_out, L0_attn_b_out)
    h = h + _L0_ffn_ref(_layernorm(h, axis=-1), L0_ffn_w_fc, L0_ffn_b_fc, L0_ffn_w_proj, L0_ffn_b_proj, L0_ffn_alpha_e, L0_ffn_alpha_r)
    return h

_drawn_inputs = setup_inputs


def setup_inputs(seed=0):
    import zlib

    import numpy as np

    out = dict(_drawn_inputs(seed))
    spreads = {'L0_tok_conv_b': (0.0, 0.1),
     'L0_tok_ln1_g': (1.0, 0.6),
     'L0_tok_ln1_b': (0.0, 0.8),
     'L0_tok_out_b': (0.0, 0.1),
     'L0_tok_ln2_g': (1.0, 0.6),
     'L0_tok_ln2_b': (0.0, 0.517),
     'L0_tok_ff1_b': (0.0, 0.346),
     'L0_tok_ff2_b': (0.0, 0.1),
     'L0_tok_lnf_g': (1.0, 0.2),
     'L0_tok_lnf_b': (0.0, 0.1),
     'L0_tok_head_b': (0.0, 0.1),
     'L0_attn_b_out': (0.0, 0.1),
     'L0_ffn_b_fc': (0.0, 0.323),
     'L0_ffn_b_proj': (0.0, 0.1)}
    factors = {'L0_tok_qkv_w': 8.0, 'L0_tok_out_w': 8.0, 'L0_ffn_alpha_r': 3.656}
    for name, (base, spread) in spreads.items():
        noise = np.random.default_rng([zlib.crc32(name.encode()), seed]).standard_normal(out[name].shape)
        drawn = base * np.exp(spread * noise) if base else spread * noise
        out[name] = jnp.asarray(drawn.astype(out[name].dtype))
    for name, factor in factors.items():
        out[name] = (out[name] * factor).astype(out[name].dtype)
    return out
```

```python
from contextlib import ExitStack

import numpy as np
import concourse.bass as bass
from concourse import mybir

F32 = mybir.dt.float32
ALU = mybir.AluOpType
ACT = mybir.ActivationFunctionType
AX_X = mybir.AxisListType.X

P = 128
IMAGES, LAYERS = 2, 2
CHANNELS, SIDE, PATCH = 32, 128, 8
TOKENS = (SIDE // PATCH) ** 2
TILES = TOKENS // P
D = 128
KCONV = CHANNELS * PATCH * PATCH // P
HEADS, DH = 8, 64
INNER = HEADS * DH
PAIRS = INNER // P
FF = 512
FC = FF // P
E = 192
EC = 96
ECH = E // EC
H3, D3 = 12, 16
HMAX = 768
HC = HMAX // P
EMBED, RATIO = (96, 144, 192), (2, 3, 4)
MIX = len(EMBED) * len(RATIO)
EPS_LN, EPS_Z = 1e-5, 1e-6
STEPS = IMAGES * LAYERS

COL = {}
for _name, _n in (("conv_b", 1), ("ln1_g", LAYERS), ("ln1_b", LAYERS), ("ln2_g", LAYERS), ("ln2_b", LAYERS),
                  ("ff1_b", LAYERS * FC), ("lnf_g", 1), ("lnf_b", 1), ("b_fc", HC)):
    COL[_name] = (sum(n for _, n in COL.values()), _n)
NCOL = sum(n for _, n in COL.values())
ROW, _at = {}, 0
for _name, _n in (("out_b", LAYERS * D), ("ff2_b", LAYERS * D), ("head_b", E), ("b_out", E), ("b_proj", E)):
    ROW[_name] = _at
    _at += _n
NROW = _at
CONV_PIECES = 4


def build(nc, small, embed0, patches1, qkv_w, rest_w, rows, mix, fc_w, proj_w, head_w, aqkv_w, aout_w, out):
    with ExitStack() as ctx:
        def sb(name, shape, dt=F32):
            return ctx.enter_context(nc.sbuf_tensor(name, shape, dt))

        def sem(name):
            return ctx.enter_context(nc.semaphore(name))

        def sems(name):
            return [sem(f"{name}{i}") for i in range(IMAGES)]

        def per_image(name, shape):
            return [sb(f"{name}{i}", shape) for i in range(IMAGES)]

        small_sb = sb("small_sb", [P, P + EC + NCOL])
        ident = small_sb[:, 0:P]
        headmask = small_sb[0:EC, P:P + EC]

        def col(name, n=0, parts=P):
            at = P + EC + COL[name][0] + n
            return small_sb[0:parts, at:at + 1]

        embed_sb = sb("embed_sb", [P, KCONV, D + TOKENS])
        patches1_sb = sb("patches1_sb", [P, KCONV, TOKENS])
        qkvw = [sb(f"qkvw{l}", [P, 3 * INNER]) for l in range(LAYERS)]
        restw = [sb(f"restw{l}", [P, PAIRS * D + FF + FC * D]) for l in range(LAYERS)]
        rows_sb = sb("rows_sb", [P, NROW])
        mix_sb = sb("mix_sb", [MIX, HMAX + E + 2])
        mask_h, mask_e = mix_sb[:, 0:HMAX], mix_sb[:, HMAX:HMAX + E]
        alpha_e, alpha_r = mix_sb[:, HMAX + E:HMAX + E + 1], mix_sb[:, HMAX + E + 1:HMAX + E + 2]
        fcw_raw = sb("fcw_raw", [EC, ECH, HMAX])
        projw_raw = sb("projw_raw", [P, HC, E])
        headw = sb("headw", [P, E])
        aqkvw = sb("aqkvw", [EC, ECH, 3 * E])
        aoutw = sb("aoutw", [EC, ECH, E])
        ones = sb("ones", [P, P])
        minus_half = sb("minus_half", [P, TILES])
        alpha = sb("alpha", [MIX, P])
        alpha_mask_e = sb("alpha_mask_e", [MIX, E])
        fc_mix = sb("fc_mix", [EC, ECH, HMAX])
        proj_mix = sb("proj_mix", [P, HC, E])
        fcw, projw = fc_mix, proj_mix
        fcb = sb("fcb", [P, HC])
        projb = sb("projb", [P, E])

        def outw(l, p):
            return restw[l][:, p * D:(p + 1) * D]

        def ff1w(l, c):
            at = PAIRS * D + c * P
            return restw[l][:, at:at + P]

        def ff2w(l, c):
            at = PAIRS * D + FF + c * D
            return restw[l][:, at:at + D]

        embT = per_image("embT", [P, TOKENS])
        x = per_image("x", [P, TILES, D])
        xb = per_image("xb", [P, TILES, D])
        h = per_image("h", [P, TILES, E])
        hb = per_image("hb", [P, TILES, E])
        stats = per_image("stats", [P, TILES, 6])
        mv = per_image("mv", [P, TILES, 2])
        var = per_image("var", [P, TILES])
        rstd = per_image("rstd", [P, TILES])
        xn = per_image("xn", [P, TILES, E])
        yT = per_image("yT", [P, TOKENS])
        yT3 = per_image("yT3", [EC, ECH, TOKENS])
        nkmax = per_image("nkmax", [P, PAIRS])
        kexp = per_image("kexp", [P, PAIRS, TOKENS])
        ksum = per_image("ksum", [P, PAIRS])
        rksum = per_image("rksum", [P, PAIRS])
        ktok = per_image("ktok", [P, TILES, INNER])
        vtok = per_image("vtok", [P, TILES, INNER])
        nqmax = per_image("nqmax", [P, TILES, HEADS])
        q = per_image("q", [P, TILES, INNER])
        qsum = per_image("qsum", [P, TILES, HEADS])
        rqsum = per_image("rqsum", [P, TILES, HEADS])
        qn = per_image("qn", [P, TILES, INNER])
        qT = per_image("qT", [P, TILES, INNER])
        ctxbd = per_image("ctxbd", [P, PAIRS, P])
        cw = per_image("cw", [P, PAIRS, D])
        hid = per_image("hid", [P, FC, TOKENS])
        qk3m = [b[:, :, 0:2 * E] for b in q]
        qk3e = [b[:].rearrange("p c t -> p (c t)").rearrange("p (t n) -> p t n", t=TILES)[:, :, 0:2 * E] for b in kexp]
        qk3 = [b[:, :, 0:2 * E] for b in ktok]
        v3 = [b[:, :, 0:E] for b in vtok]
        qks3 = [b[:, :, 0:E] for b in qT]
        qz3 = [b[:, :, 0:E] for b in qn]
        hid3 = [embed_sb[:, 4 * i:4 * i + 4, :].rearrange("p c n -> p (c n)").rearrange("p (c t) -> p c t", c=HC)
                for i in range(IMAGES)]
        kv3 = per_image("kv3", [EC, ECH, EC])
        ksum3 = per_image("ksum3", [P, E])
        den3 = per_image("den3", [P, TILES, H3])
        z3 = per_image("z3", [P, TILES, H3])
        qzT3 = per_image("qzT3", [EC, ECH, TOKENS])
        cw3 = per_image("cw3", [EC, ECH, E])
        outs = per_image("outs", [P, TILES, E])

        bank = [ctx.enter_context(nc.psum_tensor(f"bank{i}", [P, 512], F32)) for i in range(8)]
        KB, QB, VB = bank[0:2], bank[2:4], bank[4:6]
        SB_, CB = bank[6], bank[7]

        loaded = {n: sem(f"loaded_{n}") for n in (
            ["small", "mix", "rows", "fc", "proj", "head", "aqkv", "aout", "patches1a", "patches1b"]
            + [f"embed{j}" for j in range(CONV_PIECES)]
            + [f"qkv{l}" for l in range(LAYERS)] + [f"rest{l}" for l in range(LAYERS)])}
        consts_set = sem("consts_set")
        zeroed = sem("zeroed")
        alpha_ready = sem("alpha_ready")
        mix_psum = sem("mix_psum")
        mix_copied = sem("mix_copied")
        mixed_weights = sem("mixed_weights")
        conv_done, embT_ready, emb_turned, x_ready = (sems(n) for n in ("conv_done", "embT_ready", "emb_turned", "x_ready"))
        stats_done, mv_done, var_ready, rstd_ready, xn_ready, turned, yT_ready = (
            sems(n) for n in ("stats_done", "mv_done", "var_ready", "rstd_ready", "xn_ready", "turned", "yT_ready"))
        xb_ready, k_done, nkmax_ready, kexp_ready, k_turned, ktok_ready = (
            sems(n) for n in ("xb_ready", "k_done", "nkmax_ready", "kexp_ready", "k_turned", "ktok_ready"))
        v_done, vtok_ready, q_done, nqmax_ready, qsub_ready, qexp_ready, qsum_ready, rqsum_ready, qn_ready = (
            sems(n) for n in ("v_done", "vtok_ready", "q_done", "nqmax_ready", "qsub_ready", "qexp_ready",
                              "qsum_ready", "rqsum_ready", "qn_ready"))
        q_turned, qT_ready, ctx_done, ctxbd_ready, cw_done, rksum_ready, cw_ready, att_done = (
            sems(n) for n in ("q_turned", "qT_ready", "ctx_done", "ctxbd_ready", "cw_done", "rksum_ready",
                              "cw_ready", "att_done"))
        x_mid, ff1_done, hid_ready, ff2_done, x_new = (
            sems(n) for n in ("x_mid", "ff1_done", "hid_ready", "ff2_done", "x_new"))
        h_ready, hb_ready, h2_ready, outs_ready, stored = (
            sems(n) for n in ("h_ready", "hb_ready", "h2_ready", "outs_ready", "stored"))
        head_done, qk3_done, v3_done, qk3m_ready, qk3e_ready, qk3_ready, v3_ready = (
            sem(n) for n in ("head_done", "qk3_done", "v3_done", "qk3m_ready", "qk3e_ready", "qk3_ready", "v3_ready"))
        kv3_done, kv3_ready, ksum3_ready, qks3_ready, den3_sum, den3_ready, z3_ready, qz3_ready = (
            sem(n) for n in ("kv3_done", "kv3_ready", "ksum3_ready", "qks3_ready", "den3_sum", "den3_ready",
                             "z3_ready", "qz3_ready"))
        cw3_done, cw3_ready, qz3_turned, qzT3_ready, out3_done, fc_done, hid3_ready, proj_done = (
            sem(n) for n in ("cw3_done", "cw3_ready", "qz3_turned", "qzT3_ready", "out3_done", "fc_done",
                             "hid3_ready", "proj_done"))

        def LN1(l):
            return 2 * l

        def LN2(l):
            return 2 * l + 1

        LNF, LN3, LN4 = 2 * LAYERS, 2 * LAYERS + 1, 2 * LAYERS + 2

        block = ctx.enter_context(nc.Block())

        @block.sync
        def _(sp):
            sp.dma_start(small_sb[:], small).then_inc(loaded["small"], 16)
            per = KCONV // CONV_PIECES
            for j in range(CONV_PIECES):
                sp.dma_start(embed_sb[:, j * per:(j + 1) * per, :],
                             embed0[:, j * per:(j + 1) * per, :]).then_inc(loaded[f"embed{j}"], 16)
            sp.dma_start(mix_sb[:], mix).then_inc(loaded["mix"], 16)
            sp.dma_start(qkvw[0][:], qkv_w[0]).then_inc(loaded["qkv0"], 16)
            half = KCONV // 2
            sp.dma_start(patches1_sb[:, 0:half, :], patches1[:, 0:half, :]).then_inc(loaded["patches1a"], 16)
            sp.dma_start(patches1_sb[:, half:, :], patches1[:, half:, :]).then_inc(loaded["patches1b"], 16)
            sp.dma_start(restw[0][:], rest_w[0]).then_inc(loaded["rest0"], 16)
            sp.dma_start(rows_sb[:], rows.to_broadcast([P, NROW])).then_inc(loaded["rows"], 16)
            sp.dma_start(fcw_raw[:], fc_w).then_inc(loaded["fc"], 16)
            sp.dma_start(projw_raw[:], proj_w).then_inc(loaded["proj"], 16)
            sp.dma_start(qkvw[1][:], qkv_w[1]).then_inc(loaded["qkv1"], 16)
            sp.dma_start(restw[1][:], rest_w[1]).then_inc(loaded["rest1"], 16)
            sp.dma_start(headw[:], head_w).then_inc(loaded["head"], 16)
            sp.dma_start(aqkvw[:], aqkv_w).then_inc(loaded["aqkv"], 16)
            sp.dma_start(aoutw[:], aout_w).then_inc(loaded["aout"], 16)
            for i in range(IMAGES):
                sp.wait_ge(outs_ready[i], 1)
                sp.dma_start(out[i], outs[i][:]).then_inc(stored[i], 16)
            for i in range(IMAGES):
                sp.wait_ge(stored[i], 16)

        @block.tensor
        def _(pe):
            def conv(i, dst):
                for c in range(KCONV):
                    if i == 0 and c % (KCONV // CONV_PIECES) == 0:
                        pe.wait_ge(loaded[f"embed{c // (KCONV // CONV_PIECES)}"], 16)
                    if i == 1 and c % (KCONV // 2) == 0:
                        pe.wait_ge(loaded["patches1a" if c == 0 else "patches1b"], 16)
                    rhs = embed_sb[:, c, D:] if i == 0 else patches1_sb[:, c, :]
                    mm = nc.tensor.matmul(dst[:, 0:TOKENS], embed_sb[:, c, 0:D], rhs,
                                          start=(c == 0), stop=(c == KCONV - 1))
                mm.then_inc(conv_done[i], 1)

            def embedding_to_tokens(i, dst):
                pe.wait_ge(embT_ready[i], 1)
                for t in range(TILES):
                    mm = nc.tensor.transpose(dst[:, t * D:(t + 1) * D], embT[i][:, t * P:(t + 1) * P], ident)
                mm.then_inc(emb_turned[i], 1)

            def turn_norm(i, n, dst):
                pe.wait_ge(xn_ready[i], n + 1)
                for t in range(TILES):
                    if n <= LNF:
                        mm = nc.tensor.transpose(dst[:, t * P:(t + 1) * P], xn[i][:, t, 0:D], ident)
                    else:
                        for c in range(ECH):
                            at = c * TOKENS + t * P
                            mm = nc.tensor.transpose(dst[0:EC, at:at + P], xn[i][:, t, c * EC:(c + 1) * EC], ident)
                mm.then_inc(turned[i], 1)

            def qkv(l, i):
                pe.wait_ge(loaded[f"qkv{l}"], 16)
                pe.wait_ge(yT_ready[i], LN1(l) + 1)
                for b in range(2):
                    for c in range(2):
                        at = INNER + (2 * b + c) * P
                        mm = nc.tensor.matmul(KB[b][:, c * TOKENS:(c + 1) * TOKENS], qkvw[l][:, at:at + P],
                                              yT[i][:], start=True, stop=True)
                    mm.then_inc(k_done[i], 1)
                if l + i == 0:
                    pe.wait_ge(mix_copied, 9)
                for t in range(TILES):
                    nc.tensor.matmul(QB[t][:], yT[i][:, t * P:(t + 1) * P], qkvw[l][:, 0:INNER],
                                     start=True, stop=True).then_inc(q_done[i], 1)
                if l or i:
                    pe.wait_ge(x_mid[1 - i], l + i)
                for t in range(TILES):
                    nc.tensor.matmul(VB[t][:], yT[i][:, t * P:(t + 1) * P], qkvw[l][:, 2 * INNER:3 * INNER],
                                     start=True, stop=True).then_inc(v_done[i], 1)

            def turn_k(l, i):
                pe.wait_ge(kexp_ready[i], PAIRS * (l + 1))
                for t in range(TILES):
                    for c in range(PAIRS):
                        mm = nc.tensor.transpose(KB[t][:, c * P:(c + 1) * P], kexp[i][:, c, t * P:(t + 1) * P], ident)
                    mm.then_inc(k_turned[i], 1)

            def context(l, i):
                pe.wait_ge(vtok_ready[i], TILES * (l + 1))
                pe.wait_ge(ktok_ready[i], TILES * (l + 1))
                for p in range(PAIRS):
                    for t in range(TILES):
                        mm = nc.tensor.matmul(VB[0][:, p * P:(p + 1) * P], vtok[i][:, t, p * P:(p + 1) * P],
                                              ktok[i][:, t, p * P:(p + 1) * P], start=(t == 0), stop=(t == TILES - 1))
                mm.then_inc(ctx_done[i], 1)

            def context_out(l, i):
                pe.wait_ge(loaded[f"rest{l}"], 16)
                pe.wait_ge(ctxbd_ready[i], 2 * (l + 1))
                for p in range(PAIRS):
                    mm = nc.tensor.matmul(VB[1][:, p * D:(p + 1) * D], ctxbd[i][:, p, :], outw(l, p),
                                          start=True, stop=True)
                mm.then_inc(cw_done[i], 1)

            def turn_q(l, i):
                for t in range(TILES):
                    pe.wait_ge(qn_ready[i], TILES * l + t + 1)
                    for c in range(PAIRS):
                        mm = nc.tensor.transpose(QB[t][:, c * P:(c + 1) * P], qn[i][:, t, c * P:(c + 1) * P], ident)
                    mm.then_inc(q_turned[i], 1)

            def attend(l, i):
                pe.wait_ge(cw_ready[i], l + 1)
                for t in range(TILES):
                    pe.wait_ge(qT_ready[i], TILES * l + t + 1)
                    for c in range(PAIRS):
                        mm = nc.tensor.matmul(VB[0][:, t * D:(t + 1) * D], qT[i][:, t, c * P:(c + 1) * P],
                                              cw[i][:, c, :], start=(c == 0), stop=(c == PAIRS - 1))
                mm.then_inc(att_done[i], 1)

            def ff1(l, i):
                pe.wait_ge(yT_ready[i], LN2(l) + 1)
                for c in range(FC):
                    dst = (SB_ if c < 2 else CB)
                    mm = nc.tensor.matmul(dst[:, (c % 2) * TOKENS:(c % 2 + 1) * TOKENS], ff1w(l, c), yT[i][:],
                                          start=True, stop=True)
                    if c % 2:
                        mm.then_inc(ff1_done[i], 1)

            def ff2(l, i):
                pe.wait_ge(hid_ready[i], FC * (l + 1))
                for t in range(TILES):
                    for c in range(FC):
                        mm = nc.tensor.matmul(SB_[:, t * D:(t + 1) * D], hid[i][:, c, t * P:(t + 1) * P],
                                              ff2w(l, c), start=(c == 0), stop=(c == FC - 1))
                mm.then_inc(ff2_done[i], 1)

            def mix_masks():
                pe.wait_ge(loaded["mix"], 16)
                pe.wait_ge(alpha_ready, 2)
                halfh = HMAX // 2
                for c in range(ECH):
                    for g in range(2):
                        nc.tensor.matmul(bank[2 + 2 * c + g][0:EC, 0:halfh], alpha_mask_e[:, c * EC:(c + 1) * EC],
                                         mask_h[:, g * halfh:(g + 1) * halfh],
                                         start=True, stop=True).then_inc(mix_psum, 1)
                for c in range(HC):
                    nc.tensor.matmul(bank[6][:, c:c + 1], mask_h[:, c * P:(c + 1) * P], alpha[:, 0:1],
                                     start=True, stop=True)
                nc.tensor.matmul(bank[6][:, 64:64 + E], alpha[:], mask_e, start=True, stop=True).then_inc(mix_psum, 1)
                for c in range(HC):
                    if c % 2 == 0:
                        pe.wait_ge(mix_copied, c // 2 + 1)
                    dst = bank[2 + c // 2]
                    mm = nc.tensor.matmul(dst[:, (c % 2) * E:(c % 2 + 1) * E], mask_h[:, c * P:(c + 1) * P],
                                          alpha_mask_e[:], start=True, stop=True)
                    if c % 2:
                        mm.then_inc(mix_psum, 1)

            def head(i):
                pe.wait_ge(loaded["head"], 16)
                pe.wait_ge(yT_ready[i], LNF + 1)
                for t in range(TILES):
                    mm = nc.tensor.matmul(KB[0][:, t * E:(t + 1) * E], yT[i][:, t * P:(t + 1) * P], headw[:],
                                          start=True, stop=True)
                mm.then_inc(head_done, 1)

            def qkv3(i):
                pe.wait_ge(loaded["aqkv"], 16)
                pe.wait_ge(yT_ready[i], LN3 + 1)
                for t in range(TILES):
                    for c in range(ECH):
                        mm = nc.tensor.matmul(QB[t][:, 0:2 * E], yT3[i][:, c, t * P:(t + 1) * P],
                                              aqkvw[:, c, 0:2 * E], start=(c == 0), stop=(c == ECH - 1))
                    mm.then_inc(qk3_done, 1)
                if i == 0:
                    pe.wait_ge(x_mid[1], LAYERS)
                else:
                    pe.wait_ge(h2_ready[0], 1)
                for t in range(TILES):
                    for c in range(ECH):
                        mm = nc.tensor.matmul(VB[t][:, 0:E], yT3[i][:, c, t * P:(t + 1) * P],
                                              aqkvw[:, c, 2 * E:3 * E], start=(c == 0), stop=(c == ECH - 1))
                    mm.then_inc(v3_done, 1)

            def context3(i):
                pe.wait_ge(qk3_ready, TILES * i + TILES)
                for t in range(TILES):
                    mm = nc.tensor.matmul(KB[1][:, 0:E], ones[:], qk3[i][:, t, E:2 * E],
                                          start=(t == 0), stop=(t == TILES - 1))
                mm.then_inc(kv3_done, 1)
                pe.wait_ge(v3_ready, TILES * i + TILES)
                for c in range(ECH):
                    for t in range(TILES):
                        mm = nc.tensor.matmul(KB[0][0:EC, c * EC:(c + 1) * EC], v3[i][:, t, c * EC:(c + 1) * EC],
                                              qk3[i][:, t, E + c * EC:E + (c + 1) * EC],
                                              start=(t == 0), stop=(t == TILES - 1))
                mm.then_inc(kv3_done, 1)

            def context_out3(i):
                pe.wait_ge(loaded["aout"], 16)
                pe.wait_ge(kv3_ready, i + 1)
                for c in range(ECH):
                    mm = nc.tensor.matmul(VB[0][0:EC, c * E:(c + 1) * E], kv3[i][:, c, :], aoutw[:, c, :],
                                          start=True, stop=True)
                mm.then_inc(cw3_done, 1)

            def turn_q3(i):
                pe.wait_ge(qz3_ready, i + 1)
                for t in range(TILES):
                    for c in range(ECH):
                        at = c * TOKENS + t * P
                        mm = nc.tensor.transpose(QB[0][0:EC, at:at + P], qz3[i][:, t, c * EC:(c + 1) * EC], ident)
                mm.then_inc(qz3_turned, 1)

            def attend3(i):
                pe.wait_ge(cw3_ready, i + 1)
                pe.wait_ge(qzT3_ready, i + 1)
                for t in range(TILES):
                    for c in range(ECH):
                        mm = nc.tensor.matmul(VB[1][:, t * E:(t + 1) * E], qzT3[i][:, c, t * P:(t + 1) * P],
                                              cw3[i][:, c, :], start=(c == 0), stop=(c == ECH - 1))
                mm.then_inc(out3_done, 1)

            def fc3(i, g):
                pe.wait_ge(mixed_weights, 3)
                if g == 0:
                    pe.wait_ge(yT_ready[i], LN4 + 1)
                if g == 2:
                    pe.wait_ge(hid3_ready, HC * i + 2)
                dst = (SB_, CB, SB_)[g]
                for j in range(2):
                    hc = 2 * g + j
                    for c in range(ECH):
                        mm = nc.tensor.matmul(dst[:, j * TOKENS:(j + 1) * TOKENS], fcw[:, c, hc * P:(hc + 1) * P],
                                              yT3[i][:, c, :], start=(c == 0), stop=(c == ECH - 1))
                mm.then_inc(fc_done, 1)

            def proj3(i):
                pe.wait_ge(hid3_ready, HC * i + HC)
                for t in range(TILES):
                    for c in range(HC):
                        mm = nc.tensor.matmul(CB[:, t * E:(t + 1) * E], hid3[i][:, c, t * P:(t + 1) * P],
                                              projw[:, c, :], start=(c == 0), stop=(c == HC - 1))
                mm.then_inc(proj_done, 1)

            pe.wait_ge(loaded["small"], 16)
            pe.wait_ge(consts_set, 1)
            conv(0, KB[0])
            embedding_to_tokens(0, KB[1])
            mix_masks()
            turn_norm(0, LN1(0), CB)
            for s in range(STEPS):
                l, i = divmod(s, IMAGES)
                lp, ip = divmod(s - 1, IMAGES)
                qkv(l, i)
                if s == 0:
                    conv(1, SB_)
                else:
                    turn_norm(ip, LN2(lp), SB_)
                    ff1(lp, ip)
                turn_k(l, i)
                context(l, i)
                if s == 0:
                    embedding_to_tokens(1, CB)
                else:
                    ff2(lp, ip)
                context_out(l, i)
                turn_q(l, i)
                attend(l, i)
                turn_norm(1 - i, LN1((s + 1) // 2), CB)
            head(0)
            turn_norm(1, LN2(1), SB_)
            ff1(1, 1)
            turn_norm(0, LN3, KB[1])
            qkv3(0)
            ff2(1, 1)
            context3(0)
            context_out3(0)
            turn_q3(0)
            turn_norm(1, LNF, CB)
            attend3(0)
            head(1)
            turn_norm(0, LN4, SB_)
            turn_norm(1, LN3, KB[1])
            fc3(0, 0)
            fc3(0, 1)
            qkv3(1)
            fc3(0, 2)
            context3(1)
            context_out3(1)
            proj3(0)
            turn_q3(1)
            attend3(1)
            turn_norm(1, LN4, SB_)
            for g in range(3):
                if g == 1:
                    pe.wait_ge(outs_ready[0], 1)
                fc3(1, g)
            proj3(1)

        @block.vector
        def _(dve):
            def norm_stats(i, n, src, width, ready, count):
                dve.wait_ge(ready, count)
                for t in range(TILES):
                    nc.vector.bn_stats(stats[i][:, t, :], src[:, t, 0:width]).then_inc(stats_done[i], 1)
                for t in range(TILES):
                    dve.wait_ge(stats_done[i], TILES * n + t + 1)
                    nc.vector.bn_aggr(mv[i][:, t, :], stats[i][:, t, :]).then_inc(mv_done[i], 1)
                dve.wait_ge(mv_done[i], TILES * (n + 1))
                nc.vector.tensor_scalar(var[i][:], mv[i][:, :, 1], EPS_LN, None, ALU.add).then_inc(var_ready[i], 1)

            def norm_apply(i, n, src, width):
                dve.wait_ge(rstd_ready[i], n + 1)
                for t in range(TILES):
                    last = nc.vector.tensor_scalar(xn[i][:, t, 0:width], src[:, t, 0:width], mv[i][:, t, 0:1],
                                                   rstd[i][:, t:t + 1], ALU.subtract, ALU.mult)
                last.then_inc(xn_ready[i], 1)

            def norm_out(i, n, bankof, g, b):
                dve.wait_ge(turned[i], n + 1)
                nc.vector.tensor_scalar(yT[i][:], bankof[:, 0:TOKENS], g, b, ALU.mult, ALU.add).then_inc(yT_ready[i], 1)

            def norm_out3(i, n, bankof):
                dve.wait_ge(turned[i], n + 1)
                nc.vector.tensor_copy(yT3[i][:].rearrange("p c t -> p (c t)"),
                                      bankof[0:EC, 0:ECH * TOKENS]).then_inc(yT_ready[i], 1)

            def x_from_embedding(i, bankof):
                dve.wait_ge(emb_turned[i], 1)
                nc.vector.tensor_copy(x[i][:].rearrange("p t d -> p (t d)"),
                                      bankof[:, 0:TILES * D]).then_inc(x_ready[i], 1)

            def k_max(l, i):
                for b in range(2):
                    dve.wait_ge(k_done[i], 2 * l + b + 1)
                    nc.vector.tensor_reduce(nkmax[i][:, 2 * b:2 * b + 2],
                                            KB[b][:].rearrange("p (c t) -> p c t", c=2), AX_X, ALU.max,
                                            negate=True).then_inc(nkmax_ready[i], 1)

            def q_shift(l, i, t):
                dve.wait_ge(q_done[i], TILES * l + t + 1)
                heads = QB[t][:].rearrange("p (h d) -> p h d", h=HEADS)
                nc.vector.tensor_reduce(nqmax[i][:, t, :], heads, AX_X, ALU.max,
                                        negate=True).then_inc(nqmax_ready[i], 1)
                dve.wait_ge(nqmax_ready[i], TILES * l + t + 1)
                nc.vector.tensor_tensor(q[i][:, t, :].rearrange("p (h d) -> p h d", h=HEADS), heads,
                                        nqmax[i][:, t, :].unsqueeze(2).to_broadcast([P, HEADS, DH]),
                                        ALU.add).then_inc(qsub_ready[i], 1)

            def q_sum(l, i, t):
                dve.wait_ge(qexp_ready[i], TILES * l + t + 1)
                nc.vector.tensor_reduce(qsum[i][:, t, :], q[i][:, t, :].rearrange("p (h d) -> p h d", h=HEADS),
                                        AX_X, ALU.add).then_inc(qsum_ready[i], 1)
                dve.wait_ge(qsum_ready[i], TILES * l + t + 1)
                nc.vector.reciprocal(rqsum[i][:, t, :], qsum[i][:, t, :]).then_inc(rqsum_ready[i], 1)

            def k_to_sbuf(l, i, t):
                dve.wait_ge(k_turned[i], TILES * l + t + 1)
                nc.vector.tensor_copy(ktok[i][:, t, :], KB[t][:]).then_inc(ktok_ready[i], 1)

            def k_inverse_sum(l, i):
                dve.wait_ge(kexp_ready[i], PAIRS * (l + 1))
                nc.vector.reciprocal(rksum[i][:], ksum[i][:]).then_inc(rksum_ready[i], 1)

            def context_scaled(l, i):
                dve.wait_ge(cw_done[i], l + 1)
                dve.wait_ge(rksum_ready[i], l + 1)
                nc.vector.scalar_tensor_tensor(out=cw[i][:], in0=VB[1][:].rearrange("p (c d) -> p c d", c=PAIRS),
                                               scalar=DH ** -0.5, in1=rksum[i][:].unsqueeze(2).to_broadcast([P, PAIRS, D]),
                                               op0=ALU.mult, op1=ALU.mult).then_inc(cw_ready[i], 1)

            def add_attention(l, i):
                dve.wait_ge(att_done[i], l + 1)
                dve.wait_ge(xb_ready[i], 2 * l + 1)
                nc.vector.tensor_tensor(x[i][:].rearrange("p t d -> p (t d)"), VB[0][:, 0:TILES * D],
                                        xb[i][:].rearrange("p t d -> p (t d)"), ALU.add).then_inc(x_mid[i], 1)

            def add_ff(l, i):
                dve.wait_ge(ff2_done[i], l + 1)
                dve.wait_ge(xb_ready[i], 2 * l + 2)
                nc.vector.tensor_tensor(x[i][:].rearrange("p t d -> p (t d)"), SB_[:, 0:TILES * D],
                                        xb[i][:].rearrange("p t d -> p (t d)"), ALU.add).then_inc(x_new[i], 1)

            def bias_row(name):
                return rows_sb[:, ROW[name]:ROW[name] + E].unsqueeze(1).to_broadcast([P, TILES, E])

            def h_from_head(i):
                dve.wait_ge(head_done, i + 1)
                dve.wait_ge(loaded["rows"], 16)
                nc.vector.tensor_tensor(h[i][:], KB[0][:, 0:TILES * E].rearrange("p (t e) -> p t e", t=TILES),
                                        bias_row("head_b"), ALU.add).then_inc(h_ready[i], 1)

            def phi3_min(i, t):
                dve.wait_ge(qk3_done, TILES * i + t + 1)
                nc.vector.tensor_scalar(qk3m[i][:, t, :], QB[t][:, 0:2 * E], 0.0, None,
                                        ALU.min).then_inc(qk3m_ready, 1)

            def phi3_sum(i, t):
                dve.wait_ge(qk3e_ready, TILES * i + t + 1)
                nc.vector.scalar_tensor_tensor(out=qk3[i][:, t, :], in0=QB[t][:, 0:2 * E], scalar=0.0,
                                               in1=qk3e[i][:, t, :], op0=ALU.max, op1=ALU.add).then_inc(qk3_ready, 1)

            def k3_sums(i):
                dve.wait_ge(kv3_done, 2 * i + 1)
                nc.vector.tensor_scalar(ksum3[i][:], KB[1][:, 0:E], 1.0, None, ALU.add).then_inc(ksum3_ready, 1)
                dve.wait_ge(ksum3_ready, i + 1)
                nc.vector.tensor_tensor(qks3[i], qk3[i][:, :, 0:E],
                                        ksum3[i][:].unsqueeze(1).to_broadcast([P, TILES, E]),
                                        ALU.mult).then_inc(qks3_ready, 1)
                dve.wait_ge(qks3_ready, i + 1)
                nc.vector.tensor_reduce(den3[i][:],
                                        qks3[i].rearrange("p t (h d) -> p t h d", d=D3),
                                        AX_X, ALU.add).then_inc(den3_sum, 1)
                dve.wait_ge(den3_sum, i + 1)
                nc.vector.tensor_scalar(den3[i][:], den3[i][:], EPS_Z, None, ALU.add).then_inc(den3_ready, 1)
                dve.wait_ge(den3_ready, i + 1)
                nc.vector.reciprocal(z3[i][:], den3[i][:]).then_inc(z3_ready, 1)
                dve.wait_ge(z3_ready, i + 1)
                nc.vector.tensor_tensor(qz3[i].rearrange("p t (h d) -> p t h d", d=D3), qk3_q(i),
                                        z3[i][:].unsqueeze(3).to_broadcast([P, TILES, H3, D3]), ALU.mult).then_inc(qz3_ready, 1)

            def qk3_q(i):
                return qk3[i][:, :, 0:E].rearrange("p t (h d) -> p t h d", d=D3)

            def kv3_masked(i):
                dve.wait_ge(kv3_done, 2 * i + 2)
                nc.vector.tensor_tensor(kv3[i][:], KB[0][0:EC, 0:ECH * EC].rearrange("p (c e) -> p c e", c=ECH),
                                        headmask.unsqueeze(1).to_broadcast([EC, ECH, EC]),
                                        ALU.mult).then_inc(kv3_ready, 1)

            def q3_to_sbuf(i):
                dve.wait_ge(qz3_turned, i + 1)
                nc.vector.tensor_copy(qzT3[i][:].rearrange("p c t -> p (c t)"),
                                      QB[0][0:EC, 0:ECH * TOKENS]).then_inc(qzT3_ready, 1)

            def add_attention3(i):
                dve.wait_ge(out3_done, i + 1)
                dve.wait_ge(hb_ready[i], 1)
                nc.vector.tensor_tensor(h[i][:].rearrange("p t e -> p (t e)"), VB[1][:, 0:TILES * E],
                                        hb[i][:].rearrange("p t e -> p (t e)"), ALU.add).then_inc(h2_ready[i], 1)

            def add_ff3(i):
                dve.wait_ge(proj_done, i + 1)
                dve.wait_ge(hb_ready[i], 2)
                nc.vector.tensor_tensor(outs[i][:].rearrange("p t e -> p (t e)"), CB[:, 0:TILES * E],
                                        hb[i][:].rearrange("p t e -> p (t e)"), ALU.add).then_inc(outs_ready[i], 1)

            nc.vector.memset(ones[:], 1.0).then_inc(consts_set, 1)
            nc.vector.memset(minus_half[:], -0.5).then_inc(consts_set, 1)
            for i in range(IMAGES):
                nc.vector.memset(ctxbd[i][:], 0.0).then_inc(zeroed, 1)
            dve.wait_ge(loaded["mix"], 16)
            dve.wait_ge(consts_set, 1)
            nc.vector.tensor_scalar(alpha[:], ones[0:MIX, :], alpha_e, alpha_r, ALU.mult, ALU.mult).then_inc(alpha_ready, 1)
            nc.vector.tensor_scalar(alpha_mask_e[:], mask_e, alpha_e, alpha_r, ALU.mult, ALU.mult).then_inc(alpha_ready, 1)
            x_from_embedding(0, KB[1])
            norm_stats(0, LN1(0), x[0], D, x_ready[0], 1)
            norm_apply(0, LN1(0), x[0], D)
            norm_out(0, LN1(0), CB, col("ln1_g", 0), col("ln1_b", 0))
            for s in range(STEPS):
                l, i = divmod(s, IMAGES)
                lp, ip = divmod(s - 1, IMAGES)
                if s:
                    add_attention(lp, ip)
                    norm_stats(ip, LN2(lp), x[ip], D, x_mid[ip], lp + 1)
                k_max(l, i)
                if s:
                    norm_apply(ip, LN2(lp), x[ip], D)
                q_shift(l, i, 0)
                if s:
                    norm_out(ip, LN2(lp), SB_, col("ln2_g", lp), col("ln2_b", lp))
                q_shift(l, i, 1)
                k_inverse_sum(l, i)
                for t in range(TILES):
                    q_sum(l, i, t)
                for t in range(TILES):
                    k_to_sbuf(l, i, t)
                if s:
                    add_ff(lp, ip)
                    norm_stats(ip, LN1(lp + 1), x[ip], D, x_new[ip], lp + 1)
                else:
                    x_from_embedding(1, CB)
                    norm_stats(1, LN1(0), x[1], D, x_ready[1], 1)
                context_scaled(l, i)
                norm_apply(1 - i, LN1((s + 1) // 2), x[1 - i], D)
                g, b = ("lnf_g", "lnf_b") if s == STEPS - 1 else ("ln1_g", "ln1_b")
                norm_out(1 - i, LN1((s + 1) // 2), CB, col(g, (s + 1) // 2 % LAYERS), col(b, (s + 1) // 2 % LAYERS))
            add_attention(1, 1)
            norm_stats(1, LN2(1), x[1], D, x_mid[1], LAYERS)
            h_from_head(0)
            norm_stats(0, LN3, h[0], E, h_ready[0], 1)
            norm_apply(1, LN2(1), x[1], D)
            norm_apply(0, LN3, h[0], E)
            norm_out(1, LN2(1), SB_, col("ln2_g", 1), col("ln2_b", 1))
            norm_out3(0, LN3, KB[1])
            phi3_min(0, 0)
            phi3_min(0, 1)
            phi3_sum(0, 0)
            phi3_sum(0, 1)
            add_ff(1, 1)
            norm_stats(1, LNF, x[1], D, x_new[1], LAYERS)
            k3_sums(0)
            kv3_masked(0)
            norm_apply(1, LNF, x[1], D)
            q3_to_sbuf(0)
            norm_out(1, LNF, CB, col("lnf_g"), col("lnf_b"))
            add_attention3(0)
            norm_stats(0, LN4, h[0], E, h2_ready[0], 1)
            h_from_head(1)
            norm_stats(1, LN3, h[1], E, h_ready[1], 1)
            norm_apply(0, LN4, h[0], E)
            norm_out3(0, LN4, SB_)
            norm_apply(1, LN3, h[1], E)
            norm_out3(1, LN3, KB[1])
            phi3_min(1, 0)
            phi3_min(1, 1)
            phi3_sum(1, 0)
            phi3_sum(1, 1)
            k3_sums(1)
            kv3_masked(1)
            q3_to_sbuf(1)
            add_ff3(0)
            add_attention3(1)
            norm_stats(1, LN4, h[1], E, h2_ready[1], 1)
            norm_apply(1, LN4, h[1], E)
            norm_out3(1, LN4, SB_)
            add_ff3(1)

        @block.scalar
        def _(act):
            def embedding_bias(i, bankof):
                act.wait_ge(conv_done[i], 1)
                nc.scalar.activation(embT[i][:], bankof[:, 0:TOKENS], ACT.Identity,
                                     bias=col("conv_b")).then_inc(embT_ready[i], 1)

            def copy_masks():
                halfh = HMAX // 2
                for c in range(ECH):
                    for g in range(2):
                        act.wait_ge(mix_psum, 2 * c + g + 1)
                        nc.scalar.activation(fc_mix[:, c, g * halfh:(g + 1) * halfh],
                                             bank[2 + 2 * c + g][0:EC, 0:halfh], ACT.Copy).then_inc(mix_copied, 1)
                act.wait_ge(mix_psum, 5)
                nc.scalar.activation(fcb[:], bank[6][:, 0:HC], ACT.Copy).then_inc(mix_copied, 1)
                nc.scalar.activation(projb[:], bank[6][:, 64:64 + E], ACT.Copy).then_inc(mix_copied, 1)
                for g in range(HC // 2):
                    act.wait_ge(mix_psum, 6 + g)
                    nc.scalar.activation(proj_mix[:, 2 * g:2 * g + 2, :].rearrange("p c e -> p (c e)"),
                                         bank[2 + g][:, 0:2 * E], ACT.Copy).then_inc(mix_copied, 1)

            def k_exp(l, i):
                for c in range(PAIRS):
                    act.wait_ge(nkmax_ready[i], 2 * l + c // 2 + 1)
                    nc.scalar.activation(kexp[i][:, c, :], KB[c // 2][:, (c % 2) * TOKENS:(c % 2 + 1) * TOKENS],
                                         ACT.Exp, bias=nkmax[i][:, c:c + 1],
                                         accum_out=ksum[i][:, c:c + 1]).then_inc(kexp_ready[i], 1)

            def q_exp(l, i, t):
                act.wait_ge(qsub_ready[i], TILES * l + t + 1)
                nc.scalar.activation(q[i][:, t, :], q[i][:, t, :], ACT.Exp).then_inc(qexp_ready[i], 1)

            def v_to_sbuf(l, i, t):
                act.wait_ge(v_done[i], TILES * l + t + 1)
                nc.scalar.activation(vtok[i][:, t, :], VB[t][:], ACT.Copy).then_inc(vtok_ready[i], 1)

            def context_blocks(l, i):
                act.wait_ge(ctx_done[i], l + 1)
                act.wait_ge(zeroed, IMAGES)
                for a in range(2):
                    src = VB[0][a * DH:(a + 1) * DH, :].rearrange("p (c d) -> p c d", c=PAIRS)
                    nc.scalar.activation(ctxbd[i][a * DH:(a + 1) * DH, :, a * DH:(a + 1) * DH],
                                         src[:, :, a * DH:(a + 1) * DH], ACT.Copy).then_inc(ctxbd_ready[i], 1)

            def q_to_sbuf(l, i, t):
                act.wait_ge(q_turned[i], TILES * l + t + 1)
                nc.scalar.activation(qT[i][:, t, :], QB[t][:], ACT.Copy).then_inc(qT_ready[i], 1)

            def gelu(l, i):
                for c in range(FC):
                    act.wait_ge(ff1_done[i], 2 * l + c // 2 + 1)
                    src = (SB_ if c < 2 else CB)
                    nc.scalar.activation(hid[i][:, c, :], src[:, (c % 2) * TOKENS:(c % 2 + 1) * TOKENS], ACT.Gelu,
                                         bias=col("ff1_b", l * FC + c)).then_inc(hid_ready[i], 1)

            def phi3_exp(i, t):
                act.wait_ge(qk3m_ready, TILES * i + t + 1)
                nc.scalar.activation(qk3e[i][:, t, :], qk3m[i][:, t, :], ACT.Exp).then_inc(qk3e_ready, 1)

            def v3_to_sbuf(i):
                for t in range(TILES):
                    act.wait_ge(v3_done, TILES * i + t + 1)
                    nc.scalar.activation(v3[i][:, t, :], VB[t][:, 0:E], ACT.Copy).then_inc(v3_ready, 1)

            def context3_to_sbuf(i):
                act.wait_ge(cw3_done, i + 1)
                nc.scalar.activation(cw3[i][:].rearrange("p c e -> p (c e)"), VB[0][0:EC, 0:ECH * E],
                                     ACT.Copy).then_inc(cw3_ready, 1)

            def gelu3(i):
                act.wait_ge(mixed_weights, 3)
                for hc in range(HC):
                    act.wait_ge(fc_done, HC // 2 * i + hc // 2 + 1)
                    src = (SB_, CB, SB_)[hc // 2]
                    nc.scalar.activation(hid3[i][:, hc, :], src[:, (hc % 2) * TOKENS:(hc % 2 + 1) * TOKENS],
                                         ACT.Gelu_apprx_tanh, bias=fcb[:, hc:hc + 1]).then_inc(hid3_ready, 1)

            act.wait_ge(loaded["small"], 16)
            embedding_bias(0, KB[0])
            copy_masks()
            for s in range(STEPS):
                l, i = divmod(s, IMAGES)
                lp, ip = divmod(s - 1, IMAGES)
                k_exp(l, i)
                for t in range(TILES):
                    q_exp(l, i, t)
                for t in range(TILES):
                    v_to_sbuf(l, i, t)
                if s:
                    gelu(lp, ip)
                else:
                    embedding_bias(1, SB_)
                context_blocks(l, i)
                for t in range(TILES):
                    q_to_sbuf(l, i, t)
            gelu(1, 1)
            phi3_exp(0, 0)
            phi3_exp(0, 1)
            v3_to_sbuf(0)
            context3_to_sbuf(0)
            phi3_exp(1, 0)
            phi3_exp(1, 1)
            v3_to_sbuf(1)
            gelu3(0)
            context3_to_sbuf(1)
            gelu3(1)

        @block.gpsimd
        def _(pool):
            def rsqrt(i, n):
                pool.wait_ge(var_ready[i], n + 1)
                nc.gpsimd.tensor_tensor(rstd[i][:], var[i][:], minus_half[:], ALU.pow).then_inc(rstd_ready[i], 1)

            def add_bias(i, name, l, ready, count):
                pool.wait_ge(loaded["rows"], 16)
                pool.wait_ge(ready, count)
                at = ROW[name] + l * D
                nc.gpsimd.tensor_tensor(xb[i][:], x[i][:], rows_sb[:, at:at + D].unsqueeze(1).to_broadcast([P, TILES, D]),
                                        ALU.add).then_inc(xb_ready[i], 1)

            def normalise_q(l, i, t):
                pool.wait_ge(rqsum_ready[i], TILES * l + t + 1)
                nc.gpsimd.tensor_tensor(qn[i][:, t, :].rearrange("p (h d) -> p h d", h=HEADS),
                                        q[i][:, t, :].rearrange("p (h d) -> p h d", h=HEADS),
                                        rqsum[i][:, t, :].unsqueeze(2).to_broadcast([P, HEADS, DH]),
                                        ALU.mult).then_inc(qn_ready[i], 1)

            def add_bias3(i, which, row, ready):
                pool.wait_ge(ready, 1)
                nc.gpsimd.tensor_tensor(hb[i][:], h[i][:], row.unsqueeze(1).to_broadcast([P, TILES, E]),
                                        ALU.add).then_inc(hb_ready[i], 1)

            def mix_weights():
                pool.wait_ge(mix_copied, 9)
                pool.wait_ge(loaded["rows"], 16)
                nc.gpsimd.tensor_tensor(fcb[:], fcb[:], small_sb[:, P + EC + COL["b_fc"][0]:P + EC + COL["b_fc"][0] + HC],
                                        ALU.mult)
                nc.gpsimd.tensor_tensor(projb[:], projb[:], rows_sb[:, ROW["b_proj"]:ROW["b_proj"] + E],
                                        ALU.mult).then_inc(mixed_weights, 1)
                pool.wait_ge(loaded["fc"], 16)
                nc.gpsimd.tensor_tensor(fcw[:], fcw_raw[:], fc_mix[:], ALU.mult).then_inc(mixed_weights, 1)
                pool.wait_ge(loaded["proj"], 16)
                nc.gpsimd.tensor_tensor(projw[:], projw_raw[:], proj_mix[:], ALU.mult).then_inc(mixed_weights, 1)

            pool.wait_ge(loaded["small"], 16)
            pool.wait_ge(consts_set, 2)
            rsqrt(0, LN1(0))
            for s in range(STEPS):
                l, i = divmod(s, IMAGES)
                lp, ip = divmod(s - 1, IMAGES)
                if s:
                    rsqrt(ip, LN2(lp))
                    add_bias(ip, "ff2_b", lp, x_mid[ip], lp + 1)
                for t in range(TILES):
                    normalise_q(l, i, t)
                if l == 0:
                    add_bias(i, "out_b", 0, x_ready[i], 1)
                else:
                    add_bias(i, "out_b", l, x_new[i], l)
                rsqrt(1 - i, LN1((s + 1) // 2))
                if s == 0:
                    mix_weights()
            rsqrt(1, LN2(1))
            rsqrt(0, LN3)
            add_bias(1, "ff2_b", 1, x_mid[1], LAYERS)
            add_bias3(0, "b_out", rows_sb[:, ROW["b_out"]:ROW["b_out"] + E], h_ready[0])
            rsqrt(1, LNF)
            rsqrt(0, LN4)
            rsqrt(1, LN3)
            add_bias3(0, "b_proj", projb[:], h2_ready[0])
            add_bias3(1, "b_out", rows_sb[:, ROW["b_out"]:ROW["b_out"] + E], h_ready[1])
            rsqrt(1, LN4)
            add_bias3(1, "b_proj", projb[:], h2_ready[1])


def _chunks(w, rows):
    return np.ascontiguousarray(w.reshape(w.shape[0] // rows, rows, w.shape[1]).transpose(1, 0, 2))


def kernel(**inputs):
    import concourse.bacc as bacc
    from concourse.bass_utils import run_bass_kernel_spmd

    a = {k: np.asarray(v) for k, v in inputs.items()}
    T = "L0_tok_"
    g = SIDE // PATCH
    xt = a["x"].reshape(IMAGES, CHANNELS, g, PATCH, g, PATCH).transpose(0, 1, 3, 5, 2, 4)
    xt = xt.reshape(IMAGES, KCONV * P, TOKENS)
    convT = a[T + "conv_w"].reshape(D, KCONV * P).T
    embed0 = _chunks(np.concatenate([convT, xt[0]], axis=1), P)
    patches1 = _chunks(xt[1], P)
    cols = [a[T + "conv_b"][None]]
    cols += [a[T + n] for n in ("ln1_g", "ln1_b", "ln2_g", "ln2_b")]
    cols += [a[T + "ff1_b"].reshape(LAYERS * FC, P), a[T + "lnf_g"][None], a[T + "lnf_b"][None],
             a["L0_ffn_b_fc"].reshape(HC, P)]
    headmask = np.zeros((P, EC), np.float32)
    headmask[:EC] = np.kron(np.eye(EC // D3, dtype=np.float32), np.ones((D3, D3), np.float32))
    small = np.concatenate([np.eye(P, dtype=np.float32), headmask, np.concatenate(cols).T], axis=1)
    rows = np.concatenate([a[T + "out_b"].reshape(-1), a[T + "ff2_b"].reshape(-1), a[T + "head_b"],
                           a["L0_attn_b_out"], a["L0_ffn_b_proj"]])[None]
    rest = [np.concatenate([_chunks(a[T + "out_w"][l], P).reshape(P, -1), a[T + "ff1_w"][l],
                            _chunks(a[T + "ff2_w"][l], P).reshape(P, -1)], axis=1) for l in range(LAYERS)]
    mask_h = np.array([[u < r * e for u in range(HMAX)] for e in EMBED for r in RATIO], np.float32)
    mask_e = np.array([[u < e for u in range(E)] for e in EMBED for r in RATIO], np.float32)
    alpha_e = np.repeat(a["L0_ffn_alpha_e"], len(RATIO))[:, None]
    alpha_r = np.tile(a["L0_ffn_alpha_r"], len(EMBED))[:, None]
    host = {
        "small": small, "embed0": embed0, "patches1": patches1,
        "qkv_w": a[T + "qkv_w"], "rest_w": np.stack(rest), "rows": rows,
        "mix": np.concatenate([mask_h, mask_e, alpha_e, alpha_r], axis=1),
        "fc_w": _chunks(a["L0_ffn_w_fc"].T, EC), "proj_w": _chunks(a["L0_ffn_w_proj"].T, P),
        "head_w": a[T + "head_w"], "aqkv_w": _chunks(a["L0_attn_W_qkv"], EC),
        "aout_w": _chunks(a["L0_attn_W_out"], EC),
    }
    host = {k: np.ascontiguousarray(v) for k, v in host.items()}
    nc = bacc.Bacc("TRN2", target_bir_lowering=False, num_devices=1)
    args = {k: nc.dram_tensor(f"in_{k}", v.shape, F32, kind="ExternalInput").ap() for k, v in host.items()}
    out = nc.dram_tensor("out_tokens", (IMAGES, P, TILES, E), F32, kind="ExternalOutput").ap()
    build(nc, out=out, **args)
    r = run_bass_kernel_spmd(nc, [{f"in_{k}": v for k, v in host.items()}], core_ids=[0])
    got = r.results[0]["out_tokens"]
    return np.ascontiguousarray(got.transpose(0, 2, 1, 3)).reshape(IMAGES, TOKENS, E)
```

```python
from contextlib import ExitStack

import numpy as np
import concourse.bass as bass
from concourse import mybir

F32 = mybir.dt.float32
F32R = mybir.dt.float32r
ALU = mybir.AluOpType
ACT = mybir.ActivationFunctionType
AX_X = mybir.AxisListType.X

P = 128
IMAGES, LAYERS = 2, 2
CHANNELS, SIDE, PATCH = 32, 128, 8
TOKENS = (SIDE // PATCH) ** 2
TILES = TOKENS // P
D = 128
KCONV = CHANNELS * PATCH * PATCH // P
HEADS, DH = 8, 64
INNER = HEADS * DH
PAIRS = INNER // P
FF = 512
FC = FF // P
E = 192
EC = 96
ECH = E // EC
H3, D3 = 12, 16
HMAX = 768
HC = HMAX // P
EMBED, RATIO = (96, 144, 192), (2, 3, 4)
MIX = len(EMBED) * len(RATIO)
SEG = 48
HSEG, ESEG = HMAX // SEG, E // SEG
EPS_LN, EPS_Z = 1e-5, 1e-6
STEPS = IMAGES * LAYERS

COL = {}
for _name, _n in (("conv_b", 1), ("ln1_g", LAYERS), ("ln1_b", LAYERS), ("ln2_g", LAYERS), ("ln2_b", LAYERS),
                  ("ff1_b", LAYERS * FC), ("lnf_g", 1), ("lnf_b", 1), ("b_fc", HC)):
    COL[_name] = (sum(n for _, n in COL.values()), _n)
NCOL = sum(n for _, n in COL.values())
ROW, _at = {}, 0
for _name, _n in (("out_b", LAYERS * D), ("ff2_b", LAYERS * D), ("head_b", E), ("b_out", E), ("b_proj", E)):
    ROW[_name] = _at
    _at += _n
NROW = _at
CONV_PIECES = 4


def build(nc, small, embed0, patches1, qkv_w, rest_w, rows, mix, fc_w, proj_w, head_w, aqkv_w, aout_w, out):
    with ExitStack() as ctx:
        def sb(name, shape, dt=F32):
            return ctx.enter_context(nc.sbuf_tensor(name, shape, dt))

        def sem(name):
            return ctx.enter_context(nc.semaphore(name))

        def sems(name):
            return [sem(f"{name}{i}") for i in range(IMAGES)]

        def per_image(name, shape):
            return [sb(f"{name}{i}", shape) for i in range(IMAGES)]

        def shared(name, shape):
            return [sb(name, shape)] * IMAGES

        small_sb = sb("small_sb", [P, P + EC + NCOL])
        ident = small_sb[:, 0:P]
        headmask = small_sb[0:EC, P:P + EC]

        def col(name, n=0, parts=P):
            at = P + EC + COL[name][0] + n
            return small_sb[0:parts, at:at + 1]

        embed_sb = sb("embed_sb", [P, KCONV, D + TOKENS])
        patches1_sb = sb("patches1_sb", [P, KCONV, TOKENS])
        spare = embed_sb[:].rearrange("p c n -> p (c n)")
        qkvw = [sb("qkvw0", [P, 3 * INNER]), spare[:, 0:3 * INNER]]
        aqkvw = spare[0:EC, 3 * INNER:3 * INNER + ECH * 3 * E].rearrange("p (c n) -> p c n", c=ECH)
        fc_at = 3 * INNER + ECH * 3 * E
        fcw_raw = spare[0:EC, fc_at:fc_at + ECH * HMAX].rearrange("p (c n) -> p c n", c=ECH)

        def parts(name, shape):
            return sb(f"{name}_hi", shape, F32R), sb(f"{name}_lo", shape, F32R)

        qkvw_parts = [parts(f"qkvw{l}", [P, 3 * INNER]) for l in range(LAYERS)]
        ff1w_parts = [parts(f"ff1w{l}", [P, FF]) for l in range(LAYERS)]
        aqkvw_parts = parts("aqkvw", [EC, ECH, 3 * E])
        fcw_parts = parts("fcw", [EC, ECH, HMAX])
        restw = [sb(f"restw{l}", [P, PAIRS * D + FF + FC * D]) for l in range(LAYERS)]
        rows_sb = sb("rows_sb", [P, NROW])
        mix_sb = sb("mix_sb", [MIX, HMAX + E + HSEG + ESEG + 2])
        mix_at = np.cumsum([0, HMAX, E, HSEG, ESEG, 1, 1])
        mask_h, mask_e, mask_hseg, mask_eseg, alpha_e, alpha_r = (
            mix_sb[:, int(a):int(b)] for a, b in zip(mix_at[:-1], mix_at[1:]))
        projw_raw = sb("projw_raw", [P, HC, E])
        headw = sb("headw", [P, E])
        aoutw = sb("aoutw", [EC, ECH, E])
        ones = sb("ones", [P, P])
        minus_half = sb("minus_half", [P, TILES])
        alpha = sb("alpha", [MIX, P])
        alpha_mask_e = sb("alpha_mask_e", [MIX, E])
        alpha_eseg = sb("alpha_eseg", [MIX, ESEG + 1])
        fc_mix = sb("fc_mix", [EC, ECH, HSEG])
        proj_mix = sb("proj_mix", [P, HC, ESEG + 1])
        fcw = fcw_raw
        projw = projw_raw
        fcb = sb("fcb", [P, HC])
        projb = sb("projb", [P, E])

        def outw(l, p):
            return restw[l][:, p * D:(p + 1) * D]

        def ff1w_all(l):
            return restw[l][:, PAIRS * D:PAIRS * D + FF]

        def ff2w(l, c):
            at = PAIRS * D + FF + c * D
            return restw[l][:, at:at + D]

        embT = per_image("embT", [P, TOKENS])
        x = per_image("x", [P, TILES, D])
        xb = per_image("xb", [P, TILES, D])
        h = per_image("h", [P, TILES, E])
        hb = per_image("hb", [P, TILES, E])
        stats = per_image("stats", [P, TILES, 6])
        mv = per_image("mv", [P, TILES, 2])
        var = per_image("var", [P, TILES])
        rstd = per_image("rstd", [P, TILES])
        xn = per_image("xn", [P, TILES, E])
        yT = per_image("yT", [P, TOKENS])
        yT_hi, yT_lo = (list(z) for z in zip(*(parts(f"yT{i}", [P, TOKENS]) for i in range(IMAGES))))
        yT3_hi, yT3_lo = (list(z) for z in zip(*(parts(f"yT3_{i}", [EC, ECH, TOKENS]) for i in range(IMAGES))))
        nkmax = per_image("nkmax", [P, PAIRS])
        kexp = shared("kexp", [P, PAIRS, TOKENS])
        ksum = per_image("ksum", [P, PAIRS])
        rksum = per_image("rksum", [P, PAIRS])
        ktok = shared("ktok", [P, TILES, INNER])
        vtok = shared("vtok", [P, TILES, INNER])
        nqmax = per_image("nqmax", [P, TILES, HEADS])
        q = shared("q", [P, TILES, INNER])
        qsum = per_image("qsum", [P, TILES, HEADS])
        rqsum = per_image("rqsum", [P, TILES, HEADS])
        qn = shared("qn", [P, TILES, INNER])
        qT = shared("qT", [P, TILES, INNER])
        ctxbd = shared("ctxbd", [P, PAIRS, P])
        cw = shared("cw", [P, PAIRS, D])
        hid = shared("hid", [P, FC, TOKENS])
        qk3m = [b[:, :, 0:2 * E] for b in q]
        qk3e = [b[:].rearrange("p c t -> p (c t)").rearrange("p (t n) -> p t n", t=TILES)[:, :, 0:2 * E] for b in kexp]
        qk3 = [b[:, :, 0:2 * E] for b in ktok]
        v3 = [b[:, :, 0:E] for b in vtok]
        qks3 = [b[:, :, 0:E] for b in qT]
        qz3 = [b[:, :, 0:E] for b in qn]
        hid3 = [patches1_sb[:, HC * i:HC * (i + 1), :] for i in range(IMAGES)]
        kv3 = per_image("kv3", [EC, ECH, EC])
        ksum3 = per_image("ksum3", [P, E])
        den3 = per_image("den3", [P, TILES, H3])
        z3 = per_image("z3", [P, TILES, H3])
        qzT3 = per_image("qzT3", [EC, ECH, TOKENS])
        cw3 = per_image("cw3", [EC, ECH, E])
        outs = per_image("outs", [P, TILES, E])

        bank = [ctx.enter_context(nc.psum_tensor(f"bank{i}", [P, 512], F32)) for i in range(8)]
        KB, QB, VB = bank[0:2], bank[2:4], bank[4:6]
        SB_, CB = bank[6], bank[7]

        loaded = {n: sem(f"loaded_{n}") for n in (
            ["small", "mix", "rows", "fc", "proj", "head", "aqkv", "aout", "patches1a", "patches1b"]
            + [f"embed{j}" for j in range(CONV_PIECES)]
            + [f"qkv{l}" for l in range(LAYERS)] + [f"rest{l}" for l in range(LAYERS)])}
        consts_set = sem("consts_set")
        zeroed = sem("zeroed")
        alpha_ready = sem("alpha_ready")
        mix_psum = sem("mix_psum")
        mix_copied = sem("mix_copied")
        split_hi, split_lo = ({n: sem(f"{n}_{part}") for n in ("qkv0", "qkv1", "ff1_0", "ff1_1", "aqkv", "fc")}
                              for part in ("hi", "lo"))
        fc_mixed = sem("fc_mixed")
        mixed_weights = sem("mixed_weights")
        conv_done, embT_ready, emb_turned, x_ready = (sems(n) for n in ("conv_done", "embT_ready", "emb_turned", "x_ready"))
        stats_done, mv_done, var_ready, rstd_ready, xn_ready, turned, yT_ready, yT_hi_ready, yT_lo_ready = (
            sems(n) for n in ("stats_done", "mv_done", "var_ready", "rstd_ready", "xn_ready", "turned", "yT_ready",
                              "yT_hi_ready", "yT_lo_ready"))
        xb_ready, k_done, nkmax_ready, kexp_ready, k_turned, ktok_ready, ktok_odd_ready = (
            sems(n) for n in ("xb_ready", "k_done", "nkmax_ready", "kexp_ready", "k_turned", "ktok_ready",
                              "ktok_odd_ready"))
        v_done, vtok_ready, q_done, nqmax_ready, qsub_ready, qexp_ready, qsum_ready, rqsum_ready, qn_ready = (
            sems(n) for n in ("v_done", "vtok_ready", "q_done", "nqmax_ready", "qsub_ready", "qexp_ready",
                              "qsum_ready", "rqsum_ready", "qn_ready"))
        q_turned, qT_ready, ctx_done, ctxbd_ready, cw_done, rksum_ready, cw_ready, att_done = (
            sems(n) for n in ("q_turned", "qT_ready", "ctx_done", "ctxbd_ready", "cw_done", "rksum_ready",
                              "cw_ready", "att_done"))
        x_mid, ff1_done, hid_ready, ff2_done, x_new = (
            sems(n) for n in ("x_mid", "ff1_done", "hid_ready", "ff2_done", "x_new"))
        h_ready, hb_ready, h2_ready, outs_ready, stored = (
            sems(n) for n in ("h_ready", "hb_ready", "h2_ready", "outs_ready", "stored"))
        head_done, qk3_done, v3_done, qk3m_ready, qk3e_ready, qk3_ready, v3_ready = (
            sem(n) for n in ("head_done", "qk3_done", "v3_done", "qk3m_ready", "qk3e_ready", "qk3_ready", "v3_ready"))
        kv3_done, kv3_ready, ksum3_ready, qks3_ready, den3_sum, den3_ready, z3_ready, qz3_ready = (
            sem(n) for n in ("kv3_done", "kv3_ready", "ksum3_ready", "qks3_ready", "den3_sum", "den3_ready",
                             "z3_ready", "qz3_ready"))
        cw3_done, cw3_ready, qz3_turned, qzT3_ready, out3_done, fc_done, hid3_ready, proj_done = (
            sem(n) for n in ("cw3_done", "cw3_ready", "qz3_turned", "qzT3_ready", "out3_done", "fc_done",
                             "hid3_ready", "proj_done"))

        def LN1(l):
            return 2 * l

        def LN2(l):
            return 2 * l + 1

        LNF, LN3, LN4 = 2 * LAYERS, 2 * LAYERS + 1, 2 * LAYERS + 2

        block = ctx.enter_context(nc.Block())

        @block.sync
        def _(sp):
            sp.dma_start(small_sb[:], small).then_inc(loaded["small"], 16)
            per = KCONV // CONV_PIECES
            half = KCONV // 2
            for j in range(CONV_PIECES):
                sp.dma_start(embed_sb[:, j * per:(j + 1) * per, :],
                             embed0[:, j * per:(j + 1) * per, :]).then_inc(loaded[f"embed{j}"], 16)
                if j == 0:
                    sp.dma_start(mix_sb[:], mix).then_inc(loaded["mix"], 16)
            sp.dma_start(patches1_sb[:, 0:half, :], patches1[:, 0:half, :]).then_inc(loaded["patches1a"], 16)
            sp.dma_start(qkvw[0][:], qkv_w[0]).then_inc(loaded["qkv0"], 16)
            sp.dma_start(patches1_sb[:, half:, :], patches1[:, half:, :]).then_inc(loaded["patches1b"], 16)
            sp.dma_start(restw[0][:], rest_w[0]).then_inc(loaded["rest0"], 16)
            sp.dma_start(rows_sb[:], rows.to_broadcast([P, NROW])).then_inc(loaded["rows"], 16)
            sp.dma_start(projw_raw[:], proj_w).then_inc(loaded["proj"], 16)
            sp.dma_start(restw[1][:], rest_w[1]).then_inc(loaded["rest1"], 16)
            sp.dma_start(headw[:], head_w).then_inc(loaded["head"], 16)
            sp.dma_start(aoutw[:], aout_w).then_inc(loaded["aout"], 16)
            sp.wait_ge(conv_done[0], 1)
            sp.wait_ge(conv_done[1], 1)
            sp.dma_start(qkvw[1], qkv_w[1]).then_inc(loaded["qkv1"], 16)
            sp.dma_start(aqkvw, aqkv_w).then_inc(loaded["aqkv"], 16)
            sp.dma_start(fcw_raw, fc_w).then_inc(loaded["fc"], 16)
            for i in range(IMAGES):
                sp.wait_ge(outs_ready[i], 1)
                sp.dma_start(out[i], outs[i][:]).then_inc(stored[i], 16)
            for i in range(IMAGES):
                sp.wait_ge(stored[i], 16)

        @block.tensor
        def _(pe):
            def split_product(order, dst, left, right, chunks):
                for k, (a, b) in enumerate(order):
                    for n in range(chunks):
                        mm = nc.tensor.matmul(dst, left(a, n), right(b, n), start=(k == 0 and n == 0),
                                              stop=(k == len(order) - 1 and n == chunks - 1))
                return mm

            def weight_left(dst, left, right, chunks=1):
                return split_product([(0, 0), (1, 0), (0, 1)], dst, left, right, chunks)

            def weight_right(dst, left, right, chunks=1):
                return split_product([(0, 0), (0, 1), (1, 0)], dst, left, right, chunks)

            def conv(i, dst, first=0, last=KCONV):
                for c in range(first, last):
                    if i == 0 and c % (KCONV // CONV_PIECES) == 0:
                        pe.wait_ge(loaded[f"embed{c // (KCONV // CONV_PIECES)}"], 16)
                    if i == 1 and c % (KCONV // 2) == 0:
                        pe.wait_ge(loaded["patches1a" if c == 0 else "patches1b"], 16)
                    rhs = embed_sb[:, c, D:] if i == 0 else patches1_sb[:, c, :]
                    mm = nc.tensor.matmul(dst[:, 0:TOKENS], embed_sb[:, c, 0:D], rhs,
                                          start=(c == 0), stop=(c == KCONV - 1))
                if last == KCONV:
                    mm.then_inc(conv_done[i], 1)

            def embedding_to_tokens(i, dst):
                pe.wait_ge(embT_ready[i], 1)
                for t in range(TILES):
                    mm = nc.tensor.transpose(dst[:, t * D:(t + 1) * D], embT[i][:, t * P:(t + 1) * P], ident)
                mm.then_inc(emb_turned[i], 1)

            def turn_norm(i, n, dst):
                pe.wait_ge(xn_ready[i], n + 1)
                for t in range(TILES):
                    if n <= LNF:
                        mm = nc.tensor.transpose(dst[:, t * P:(t + 1) * P], xn[i][:, t, 0:D], ident)
                    else:
                        for c in range(ECH):
                            at = c * TOKENS + t * P
                            mm = nc.tensor.transpose(dst[0:EC, at:at + P], xn[i][:, t, c * EC:(c + 1) * EC], ident)
                mm.then_inc(turned[i], 1)

            def qkv_k(l, i):
                pe.wait_ge(split_lo[f"qkv{l}"], 1)
                pe.wait_ge(yT_hi_ready[i], LN1(l) + 1)
                pe.wait_ge(yT_lo_ready[i], LN1(l) + 1)
                for b in range(2):
                    for c in range(2):
                        at = INNER + (2 * b + c) * P
                        mm = weight_left(KB[b][:, c * TOKENS:(c + 1) * TOKENS],
                                         lambda part, n: qkvw_parts[l][part][:, at:at + P],
                                         lambda part, n: (yT_hi, yT_lo)[part][i][:])
                    mm.then_inc(k_done[i], 1)

            def qkv_q(l, i):
                pe.wait_ge(split_lo[f"qkv{l}"], 2)
                for t in range(TILES):
                    weight_right(QB[t][:], lambda part, n: (yT_hi, yT_lo)[part][i][:, t * P:(t + 1) * P],
                                 lambda part, n: qkvw_parts[l][part][:, 0:INNER]).then_inc(q_done[i], 1)

            def qkv_v(l, i):
                pe.wait_ge(split_lo[f"qkv{l}"], 3)
                if l or i:
                    pe.wait_ge(x_mid[1 - i], l + i)
                for t in range(TILES):
                    weight_right(VB[t][:], lambda part, n: (yT_hi, yT_lo)[part][i][:, t * P:(t + 1) * P],
                                 lambda part, n: qkvw_parts[l][part][:, 2 * INNER:3 * INNER]).then_inc(v_done[i], 1)

            def turn_k(l, i):
                pe.wait_ge(kexp_ready[i], PAIRS * (l + 1))
                for t in range(TILES):
                    for c in range(PAIRS):
                        mm = nc.tensor.transpose(KB[t][:, c * P:(c + 1) * P], kexp[i][:, c, t * P:(t + 1) * P], ident)
                    mm.then_inc(k_turned[i], 1)

            def context(l, i):
                pe.wait_ge(vtok_ready[i], TILES * (l + 1))
                pe.wait_ge(ktok_ready[i], l + 1)
                pe.wait_ge(ktok_odd_ready[i], l + 1)
                for p in range(PAIRS):
                    for t in range(TILES):
                        mm = nc.tensor.matmul(VB[0][:, p * P:(p + 1) * P], vtok[i][:, t, p * P:(p + 1) * P],
                                              ktok[i][:, t, p * P:(p + 1) * P], start=(t == 0), stop=(t == TILES - 1))
                mm.then_inc(ctx_done[i], 1)

            def context_out(l, i):
                pe.wait_ge(loaded[f"rest{l}"], 16)
                pe.wait_ge(ctxbd_ready[i], 2 * (l + 1))
                for p in range(PAIRS):
                    mm = nc.tensor.matmul(VB[1][:, p * D:(p + 1) * D], ctxbd[i][:, p, :], outw(l, p),
                                          start=True, stop=True)
                mm.then_inc(cw_done[i], 1)

            def turn_q(l, i):
                for t in range(TILES):
                    pe.wait_ge(qn_ready[i], TILES * l + t + 1)
                    for c in range(PAIRS):
                        mm = nc.tensor.transpose(QB[t][:, c * P:(c + 1) * P], qn[i][:, t, c * P:(c + 1) * P], ident)
                    mm.then_inc(q_turned[i], 1)

            def attend(l, i, t):
                if t == 0:
                    pe.wait_ge(cw_ready[i], l + 1)
                pe.wait_ge(qT_ready[i], TILES * l + t + 1)
                for c in range(PAIRS):
                    mm = nc.tensor.matmul(VB[0][:, t * D:(t + 1) * D], qT[i][:, t, c * P:(c + 1) * P],
                                          cw[i][:, c, :], start=(c == 0), stop=(c == PAIRS - 1))
                if t == TILES - 1:
                    mm.then_inc(att_done[i], 1)

            def ff1(l, i):
                pe.wait_ge(split_lo[f"ff1_{l}"], 1)
                pe.wait_ge(yT_hi_ready[i], LN2(l) + 1)
                pe.wait_ge(yT_lo_ready[i], LN2(l) + 1)
                for c in range(FC):
                    dst = (SB_ if c < 2 else CB)
                    mm = weight_left(dst[:, (c % 2) * TOKENS:(c % 2 + 1) * TOKENS],
                                     lambda part, n: ff1w_parts[l][part][:, c * P:(c + 1) * P],
                                     lambda part, n: (yT_hi, yT_lo)[part][i][:])
                    if c % 2:
                        mm.then_inc(ff1_done[i], 1)

            def ff2(l, i):
                pe.wait_ge(hid_ready[i], FC * (l + 1))
                for t in range(TILES):
                    for c in range(FC):
                        mm = nc.tensor.matmul(SB_[:, t * D:(t + 1) * D], hid[i][:, c, t * P:(t + 1) * P],
                                              ff2w(l, c), start=(c == 0), stop=(c == FC - 1))
                mm.then_inc(ff2_done[i], 1)

            def mix_masks():
                pe.wait_ge(loaded["mix"], 16)
                pe.wait_ge(alpha_ready, 3)
                for c in range(ECH):
                    nc.tensor.matmul(SB_[0:EC, c * HSEG:(c + 1) * HSEG], alpha_mask_e[:, c * EC:(c + 1) * EC],
                                     mask_hseg, start=True, stop=True)
                for c in range(HC):
                    at = 64 + c * (ESEG + 1)
                    nc.tensor.matmul(SB_[:, at:at + ESEG + 1], mask_h[:, c * P:(c + 1) * P], alpha_eseg[:],
                                     start=True, stop=True)
                nc.tensor.matmul(SB_[:, 128:128 + E], alpha[:], mask_e, start=True, stop=True).then_inc(mix_psum, 1)

            def head(i):
                pe.wait_ge(loaded["head"], 16)
                pe.wait_ge(yT_ready[i], LNF + 1)
                if i:
                    pe.wait_ge(kv3_ready, 1)
                for t in range(TILES):
                    mm = nc.tensor.matmul(KB[0][:, t * E:(t + 1) * E], yT[i][:, t * P:(t + 1) * P], headw[:],
                                          start=True, stop=True)
                mm.then_inc(head_done, 1)

            def qkv3(i):
                pe.wait_ge(split_lo["aqkv"], 1)
                pe.wait_ge(yT_hi_ready[i], LN3)
                pe.wait_ge(yT_lo_ready[i], LN3)
                for t in range(TILES):
                    weight_right(QB[t][:, 0:2 * E],
                                 lambda part, c: (yT3_hi, yT3_lo)[part][i][:, c, t * P:(t + 1) * P],
                                 lambda part, c: aqkvw_parts[part][:, c, 0:2 * E], ECH).then_inc(qk3_done, 1)
                if i == 0:
                    pe.wait_ge(x_mid[1], LAYERS)
                else:
                    pe.wait_ge(h2_ready[0], 1)
                for t in range(TILES):
                    weight_right(VB[t][:, 0:E],
                                 lambda part, c: (yT3_hi, yT3_lo)[part][i][:, c, t * P:(t + 1) * P],
                                 lambda part, c: aqkvw_parts[part][:, c, 2 * E:3 * E], ECH).then_inc(v3_done, 1)

            def context3(i):
                pe.wait_ge(qk3_ready, TILES * i + TILES)
                for t in range(TILES):
                    mm = nc.tensor.matmul(KB[1][:, 0:E], ones[:], qk3[i][:, t, E:2 * E],
                                          start=(t == 0), stop=(t == TILES - 1))
                mm.then_inc(kv3_done, 1)
                pe.wait_ge(v3_ready, TILES * i + TILES)
                for c in range(ECH):
                    for t in range(TILES):
                        mm = nc.tensor.matmul(KB[0][0:EC, c * EC:(c + 1) * EC], v3[i][:, t, c * EC:(c + 1) * EC],
                                              qk3[i][:, t, E + c * EC:E + (c + 1) * EC],
                                              start=(t == 0), stop=(t == TILES - 1))
                mm.then_inc(kv3_done, 1)

            def context_out3(i):
                pe.wait_ge(loaded["aout"], 16)
                pe.wait_ge(kv3_ready, i + 1)
                for c in range(ECH):
                    mm = nc.tensor.matmul(VB[0][0:EC, c * E:(c + 1) * E], kv3[i][:, c, :], aoutw[:, c, :],
                                          start=True, stop=True)
                mm.then_inc(cw3_done, 1)

            def turn_q3(i):
                pe.wait_ge(qz3_ready, i + 1)
                for t in range(TILES):
                    for c in range(ECH):
                        at = c * TOKENS + t * P
                        mm = nc.tensor.transpose(QB[0][0:EC, at:at + P], qz3[i][:, t, c * EC:(c + 1) * EC], ident)
                mm.then_inc(qz3_turned, 1)

            def attend3(i):
                pe.wait_ge(cw3_ready, i + 1)
                pe.wait_ge(qzT3_ready, i + 1)
                for t in range(TILES):
                    for c in range(ECH):
                        mm = nc.tensor.matmul(VB[1][:, t * E:(t + 1) * E], qzT3[i][:, c, t * P:(t + 1) * P],
                                              cw3[i][:, c, :], start=(c == 0), stop=(c == ECH - 1))
                mm.then_inc(out3_done, 1)

            def fc3(i, g):
                if g == 0:
                    pe.wait_ge(split_lo["fc"], ECH)
                    pe.wait_ge(yT_hi_ready[i], LN4)
                    pe.wait_ge(yT_lo_ready[i], LN4)
                if g == 2:
                    pe.wait_ge(hid3_ready, HC * i + 2)
                dst = (SB_, CB, SB_)[g]
                for j in range(2):
                    hc = 2 * g + j
                    mm = weight_left(dst[:, j * TOKENS:(j + 1) * TOKENS],
                                     lambda part, c: fcw_parts[part][:, c, hc * P:(hc + 1) * P],
                                     lambda part, c: (yT3_hi, yT3_lo)[part][i][:, c, :], ECH)
                mm.then_inc(fc_done, 1)

            def proj3(i):
                pe.wait_ge(mixed_weights, 2)
                pe.wait_ge(hid3_ready, HC * i + HC)
                for t in range(TILES):
                    for c in range(HC):
                        mm = nc.tensor.matmul(CB[:, t * E:(t + 1) * E], hid3[i][:, c, t * P:(t + 1) * P],
                                              projw[:, c, :], start=(c == 0), stop=(c == HC - 1))
                mm.then_inc(proj_done, 1)

            half = KCONV // 2
            pe.wait_ge(loaded["small"], 16)
            pe.wait_ge(consts_set, 1)
            conv(0, KB[0])
            mix_masks()
            embedding_to_tokens(0, KB[1])
            conv(1, QB[0], 0, half)
            turn_norm(0, LN1(0), CB)
            for s in range(STEPS):
                l, i = divmod(s, IMAGES)
                lp, ip = divmod(s - 1, IMAGES)
                if s == 0:
                    conv(1, QB[0], half, KCONV)
                qkv_k(l, i)
                if s == 0:
                    pe.wait_ge(embT_ready[1], 1)
                qkv_q(l, i)
                if s:
                    turn_norm(ip, LN2(lp), SB_)
                else:
                    embedding_to_tokens(1, CB)
                qkv_v(l, i)
                if s:
                    ff1(lp, ip)
                turn_k(l, i)
                context(l, i)
                if s:
                    ff2(lp, ip)
                context_out(l, i)
                turn_q(l, i)
                attend(l, i, 0)
                turn_norm(1 - i, LN1((s + 1) // 2), CB)
                attend(l, i, 1)
            head(0)
            turn_norm(1, LN2(1), SB_)
            ff1(1, 1)
            turn_norm(0, LN3, KB[1])
            ff2(1, 1)
            qkv3(0)
            turn_norm(1, LNF, CB)
            context3(0)
            head(1)
            context_out3(0)
            turn_q3(0)
            attend3(0)
            turn_norm(1, LN3, KB[1])
            qkv3(1)
            turn_norm(0, LN4, SB_)
            context3(1)
            context_out3(1)
            fc3(0, 0)
            fc3(0, 1)
            turn_q3(1)
            attend3(1)
            fc3(0, 2)
            proj3(0)
            turn_norm(1, LN4, SB_)
            for g in range(3):
                if g == 1:
                    pe.wait_ge(outs_ready[0], 1)
                fc3(1, g)
            proj3(1)

        @block.vector
        def _(dve):
            def norm_stats(i, n, src, width, ready, count):
                dve.wait_ge(ready, count)
                for t in range(TILES):
                    nc.vector.bn_stats(stats[i][:, t, :], src[:, t, 0:width]).then_inc(stats_done[i], 1)
                for t in range(TILES):
                    dve.wait_ge(stats_done[i], TILES * n + t + 1)
                    nc.vector.bn_aggr(mv[i][:, t, :], stats[i][:, t, :]).then_inc(mv_done[i], 1)
                dve.wait_ge(mv_done[i], TILES * (n + 1))
                nc.vector.tensor_scalar(var[i][:], mv[i][:, :, 1], EPS_LN, None, ALU.add).then_inc(var_ready[i], 1)

            def norm_apply(i, n, src, width):
                dve.wait_ge(rstd_ready[i], n + 1)
                for t in range(TILES):
                    last = nc.vector.tensor_scalar(xn[i][:, t, 0:width], src[:, t, 0:width], mv[i][:, t, 0:1],
                                                   rstd[i][:, t:t + 1], ALU.subtract, ALU.mult)
                last.then_inc(xn_ready[i], 1)

            def norm_out(i, n, bankof, g, b):
                dve.wait_ge(turned[i], n + 1)
                nc.vector.tensor_scalar(yT[i][:], bankof[:, 0:TOKENS], g, b, ALU.mult, ALU.add).then_inc(yT_ready[i], 1)

            def norm_out_hi(i, n):
                dve.wait_ge(yT_ready[i], n + 1)
                nc.vector.tensor_copy(yT_hi[i][:], yT[i][:]).then_inc(yT_hi_ready[i], 1)

            def norm_out_lo(i, n):
                dve.wait_ge(yT_hi_ready[i], n + 1)
                nc.vector.tensor_tensor(yT_lo[i][:], yT[i][:], yT_hi[i][:].bitcast(F32),
                                        ALU.subtract).then_inc(yT_lo_ready[i], 1)

            def norm_out3(i, n, bankof):
                dve.wait_ge(turned[i], n + 1)
                src = bankof[0:EC, 0:ECH * TOKENS].rearrange("p (c t) -> p c t", c=ECH)
                nc.vector.tensor_copy(yT3_hi[i][:], src).then_inc(yT_hi_ready[i], 1)
                dve.wait_ge(yT_hi_ready[i], n)
                nc.vector.tensor_tensor(yT3_lo[i][:], src, yT3_hi[i][:].bitcast(F32),
                                        ALU.subtract).then_inc(yT_lo_ready[i], 1)

            def weight_low_part(name, n, raw, hi, lo):
                dve.wait_ge(split_hi[name], n)
                nc.vector.tensor_tensor(lo, raw, hi.bitcast(F32), ALU.subtract).then_inc(split_lo[name], 1)

            def x_from_embedding(i, bankof):
                dve.wait_ge(emb_turned[i], 1)
                nc.vector.tensor_copy(x[i][:].rearrange("p t d -> p (t d)"),
                                      bankof[:, 0:TILES * D]).then_inc(x_ready[i], 1)

            def k_max(l, i):
                for b in range(2):
                    dve.wait_ge(k_done[i], 2 * l + b + 1)
                    nc.vector.tensor_reduce(nkmax[i][:, 2 * b:2 * b + 2],
                                            KB[b][:].rearrange("p (c t) -> p c t", c=2), AX_X, ALU.max,
                                            negate=True).then_inc(nkmax_ready[i], 1)

            def q_max(l, i, t):
                dve.wait_ge(q_done[i], TILES * l + t + 1)
                nc.vector.tensor_reduce(nqmax[i][:, t, :], QB[t][:].rearrange("p (h d) -> p h d", h=HEADS),
                                        AX_X, ALU.max, negate=True).then_inc(nqmax_ready[i], 1)

            def q_shift(l, i, t):
                dve.wait_ge(nqmax_ready[i], TILES * l + t + 1)
                nc.vector.tensor_tensor(q[i][:, t, :].rearrange("p (h d) -> p h d", h=HEADS),
                                        QB[t][:].rearrange("p (h d) -> p h d", h=HEADS),
                                        nqmax[i][:, t, :].unsqueeze(2).to_broadcast([P, HEADS, DH]),
                                        ALU.add).then_inc(qsub_ready[i], 1)

            def q_sum(l, i, t):
                dve.wait_ge(qexp_ready[i], TILES * l + t + 1)
                nc.vector.tensor_reduce(qsum[i][:, t, :], q[i][:, t, :].rearrange("p (h d) -> p h d", h=HEADS),
                                        AX_X, ALU.add).then_inc(qsum_ready[i], 1)

            def q_inverse_sum(l, i, t):
                dve.wait_ge(qsum_ready[i], TILES * l + t + 1)
                nc.vector.reciprocal(rqsum[i][:, t, :], qsum[i][:, t, :]).then_inc(rqsum_ready[i], 1)

            def k_to_sbuf(l, i, t):
                dve.wait_ge(k_turned[i], TILES * l + 1)
                nc.vector.tensor_copy(ktok[i][:, t, :], KB[t][:]).then_inc(ktok_ready[i], 1)

            def k_inverse_sum(l, i):
                dve.wait_ge(kexp_ready[i], PAIRS * (l + 1))
                nc.vector.reciprocal(rksum[i][:], ksum[i][:]).then_inc(rksum_ready[i], 1)

            def context_scaled(l, i):
                dve.wait_ge(cw_done[i], l + 1)
                dve.wait_ge(rksum_ready[i], l + 1)
                nc.vector.scalar_tensor_tensor(out=cw[i][:], in0=VB[1][:].rearrange("p (c d) -> p c d", c=PAIRS),
                                               scalar=DH ** -0.5, in1=rksum[i][:].unsqueeze(2).to_broadcast([P, PAIRS, D]),
                                               op0=ALU.mult, op1=ALU.mult).then_inc(cw_ready[i], 1)

            def add_attention(l, i):
                dve.wait_ge(att_done[i], l + 1)
                dve.wait_ge(xb_ready[i], 2 * l + 1)
                nc.vector.tensor_tensor(x[i][:].rearrange("p t d -> p (t d)"), VB[0][:, 0:TILES * D],
                                        xb[i][:].rearrange("p t d -> p (t d)"), ALU.add).then_inc(x_mid[i], 1)

            def add_ff(l, i):
                dve.wait_ge(ff2_done[i], l + 1)
                dve.wait_ge(xb_ready[i], 2 * l + 2)
                nc.vector.tensor_tensor(x[i][:].rearrange("p t d -> p (t d)"), SB_[:, 0:TILES * D],
                                        xb[i][:].rearrange("p t d -> p (t d)"), ALU.add).then_inc(x_new[i], 1)

            def bias_row(name):
                return rows_sb[:, ROW[name]:ROW[name] + E].unsqueeze(1).to_broadcast([P, TILES, E])

            def h_from_head(i):
                dve.wait_ge(head_done, i + 1)
                dve.wait_ge(loaded["rows"], 16)
                nc.vector.tensor_tensor(h[i][:], KB[0][:, 0:TILES * E].rearrange("p (t e) -> p t e", t=TILES),
                                        bias_row("head_b"), ALU.add).then_inc(h_ready[i], 1)

            def phi3_min(i, t):
                dve.wait_ge(qk3_done, TILES * i + t + 1)
                nc.vector.tensor_scalar(qk3m[i][:, t, :], QB[t][:, 0:2 * E], 0.0, None,
                                        ALU.min).then_inc(qk3m_ready, 1)

            def phi3_sum(i, t):
                dve.wait_ge(qk3e_ready, TILES * i + t + 1)
                nc.vector.scalar_tensor_tensor(out=qk3[i][:, t, :], in0=QB[t][:, 0:2 * E], scalar=0.0,
                                               in1=qk3e[i][:, t, :], op0=ALU.max, op1=ALU.add).then_inc(qk3_ready, 1)

            def k3_sums(i):
                dve.wait_ge(kv3_done, 2 * i + 1)
                nc.vector.tensor_scalar(ksum3[i][:], KB[1][:, 0:E], 1.0, None, ALU.add).then_inc(ksum3_ready, 1)
                dve.wait_ge(ksum3_ready, i + 1)
                nc.vector.tensor_tensor(qks3[i], qk3[i][:, :, 0:E],
                                        ksum3[i][:].unsqueeze(1).to_broadcast([P, TILES, E]),
                                        ALU.mult).then_inc(qks3_ready, 1)
                dve.wait_ge(qks3_ready, i + 1)
                nc.vector.tensor_reduce(den3[i][:],
                                        qks3[i].rearrange("p t (h d) -> p t h d", d=D3),
                                        AX_X, ALU.add).then_inc(den3_sum, 1)
                dve.wait_ge(den3_sum, i + 1)
                nc.vector.tensor_scalar(den3[i][:], den3[i][:], EPS_Z, None, ALU.add).then_inc(den3_ready, 1)

            def z3_apply(i):
                dve.wait_ge(den3_ready, i + 1)
                nc.vector.reciprocal(z3[i][:], den3[i][:]).then_inc(z3_ready, 1)
                dve.wait_ge(z3_ready, i + 1)
                nc.vector.tensor_tensor(qz3[i].rearrange("p t (h d) -> p t h d", d=D3), qk3_q(i),
                                        z3[i][:].unsqueeze(3).to_broadcast([P, TILES, H3, D3]), ALU.mult).then_inc(qz3_ready, 1)

            def qk3_q(i):
                return qk3[i][:, :, 0:E].rearrange("p t (h d) -> p t h d", d=D3)

            def kv3_masked(i):
                dve.wait_ge(kv3_done, 2 * i + 2)
                nc.vector.tensor_tensor(kv3[i][:], KB[0][0:EC, 0:ECH * EC].rearrange("p (c e) -> p c e", c=ECH),
                                        headmask.unsqueeze(1).to_broadcast([EC, ECH, EC]),
                                        ALU.mult).then_inc(kv3_ready, 1)

            def q3_to_sbuf(i):
                dve.wait_ge(qz3_turned, i + 1)
                nc.vector.tensor_copy(qzT3[i][:].rearrange("p c t -> p (c t)"),
                                      QB[0][0:EC, 0:ECH * TOKENS]).then_inc(qzT3_ready, 1)

            def add_attention3(i):
                dve.wait_ge(out3_done, i + 1)
                dve.wait_ge(hb_ready[i], 1)
                nc.vector.tensor_tensor(h[i][:].rearrange("p t e -> p (t e)"), VB[1][:, 0:TILES * E],
                                        hb[i][:].rearrange("p t e -> p (t e)"), ALU.add).then_inc(h2_ready[i], 1)

            def add_ff3(i):
                dve.wait_ge(proj_done, i + 1)
                dve.wait_ge(hb_ready[i], 2)
                nc.vector.tensor_tensor(outs[i][:].rearrange("p t e -> p (t e)"), CB[:, 0:TILES * E],
                                        hb[i][:].rearrange("p t e -> p (t e)"), ALU.add).then_inc(outs_ready[i], 1)

            nc.vector.memset(ones[:], 1.0).then_inc(consts_set, 1)
            nc.vector.memset(minus_half[:], -0.5).then_inc(consts_set, 1)
            nc.vector.memset(ctxbd[0][:], 0.0).then_inc(zeroed, 1)
            dve.wait_ge(loaded["mix"], 16)
            dve.wait_ge(consts_set, 1)
            nc.vector.tensor_scalar(alpha[:], ones[0:MIX, :], alpha_e, alpha_r, ALU.mult, ALU.mult).then_inc(alpha_ready, 1)
            nc.vector.tensor_scalar(alpha_mask_e[:], mask_e, alpha_e, alpha_r, ALU.mult, ALU.mult).then_inc(alpha_ready, 1)
            nc.vector.tensor_scalar(alpha_eseg[:, 0:ESEG], mask_eseg, alpha_e, alpha_r, ALU.mult, ALU.mult)
            nc.vector.tensor_scalar(alpha_eseg[:, ESEG:], ones[0:MIX, 0:1], alpha_e, alpha_r,
                                    ALU.mult, ALU.mult).then_inc(alpha_ready, 1)
            x_from_embedding(0, KB[1])
            norm_stats(0, LN1(0), x[0], D, x_ready[0], 1)
            for n, third in enumerate((1, 0, 2)):
                at = slice(third * INNER, (third + 1) * INNER)
                weight_low_part("qkv0", n + 1, qkvw[0][:, at], qkvw_parts[0][0][:, at], qkvw_parts[0][1][:, at])
            norm_apply(0, LN1(0), x[0], D)
            norm_out(0, LN1(0), CB, col("ln1_g", 0), col("ln1_b", 0))
            norm_out_hi(0, LN1(0))
            norm_out_lo(0, LN1(0))
            for s in range(STEPS):
                l, i = divmod(s, IMAGES)
                lp, ip = divmod(s - 1, IMAGES)
                if s:
                    add_attention(lp, ip)
                    norm_stats(ip, LN2(lp), x[ip], D, x_mid[ip], lp + 1)
                k_max(l, i)
                if s:
                    norm_apply(ip, LN2(lp), x[ip], D)
                q_max(l, i, 0)
                if s:
                    norm_out(ip, LN2(lp), SB_, col("ln2_g", lp), col("ln2_b", lp))
                q_shift(l, i, 0)
                if s:
                    norm_out_hi(ip, LN2(lp))
                q_max(l, i, 1)
                if s:
                    norm_out_lo(ip, LN2(lp))
                q_shift(l, i, 1)
                if s == 0:
                    x_from_embedding(1, CB)
                q_sum(l, i, 0)
                k_to_sbuf(l, i, 0)
                q_inverse_sum(l, i, 0)
                q_sum(l, i, 1)
                k_inverse_sum(l, i)
                q_inverse_sum(l, i, 1)
                if s:
                    add_ff(lp, ip)
                    norm_stats(ip, LN1(lp + 1), x[ip], D, x_new[ip], lp + 1)
                else:
                    norm_stats(1, LN1(0), x[1], D, x_ready[1], 1)
                context_scaled(l, i)
                norm_apply(1 - i, LN1((s + 1) // 2), x[1 - i], D)
                last = s == STEPS - 1
                g, b = ("lnf_g", "lnf_b") if last else ("ln1_g", "ln1_b")
                norm_out(1 - i, LN1((s + 1) // 2), CB, col(g, (s + 1) // 2 % LAYERS), col(b, (s + 1) // 2 % LAYERS))
                if not last:
                    norm_out_hi(1 - i, LN1((s + 1) // 2))
                    norm_out_lo(1 - i, LN1((s + 1) // 2))
            add_attention(1, 1)
            norm_stats(1, LN2(1), x[1], D, x_mid[1], LAYERS)
            h_from_head(0)
            norm_stats(0, LN3, h[0], E, h_ready[0], 1)
            norm_apply(1, LN2(1), x[1], D)
            norm_out(1, LN2(1), SB_, col("ln2_g", 1), col("ln2_b", 1))
            norm_out_hi(1, LN2(1))
            norm_out_lo(1, LN2(1))
            norm_apply(0, LN3, h[0], E)
            norm_out3(0, LN3, KB[1])
            add_ff(1, 1)
            norm_stats(1, LNF, x[1], D, x_new[1], LAYERS)
            for t in range(TILES):
                phi3_min(0, t)
            norm_apply(1, LNF, x[1], D)
            norm_out(1, LNF, CB, col("lnf_g"), col("lnf_b"))
            for t in range(TILES):
                phi3_sum(0, t)
            kv3_masked(0)
            k3_sums(0)
            h_from_head(1)
            norm_stats(1, LN3, h[1], E, h_ready[1], 1)
            z3_apply(0)
            norm_apply(1, LN3, h[1], E)
            q3_to_sbuf(0)
            norm_out3(1, LN3, KB[1])
            add_attention3(0)
            norm_stats(0, LN4, h[0], E, h2_ready[0], 1)
            for t in range(TILES):
                phi3_min(1, t)
            norm_apply(0, LN4, h[0], E)
            for t in range(TILES):
                phi3_sum(1, t)
            norm_out3(0, LN4, SB_)
            kv3_masked(1)
            k3_sums(1)
            z3_apply(1)
            q3_to_sbuf(1)
            add_attention3(1)
            norm_stats(1, LN4, h[1], E, h2_ready[1], 1)
            norm_apply(1, LN4, h[1], E)
            add_ff3(0)
            norm_out3(1, LN4, SB_)
            add_ff3(1)

        @block.scalar
        def _(act):
            def embedding_bias(i, bankof):
                act.wait_ge(conv_done[i], 1)
                nc.scalar.activation(embT[i][:], bankof[:, 0:TOKENS], ACT.Identity,
                                     bias=col("conv_b")).then_inc(embT_ready[i], 1)

            def copy_masks():
                act.wait_ge(mix_psum, 1)
                nc.scalar.activation(fc_mix[:].rearrange("p c s -> p (c s)"), SB_[0:EC, 0:ECH * HSEG],
                                     ACT.Copy).then_inc(mix_copied, 1)
                nc.scalar.activation(proj_mix[:].rearrange("p c s -> p (c s)"), SB_[:, 64:64 + HC * (ESEG + 1)],
                                     ACT.Copy).then_inc(mix_copied, 1)
                nc.scalar.activation(projb[:], SB_[:, 128:128 + E], ACT.Copy).then_inc(mix_copied, 1)

            def weight_high_part(name, raw, hi):
                nc.scalar.activation(hi, raw, ACT.Copy).then_inc(split_hi[name], 1)

            def k_exp(l, i):
                for c in range(PAIRS):
                    act.wait_ge(nkmax_ready[i], 2 * l + c // 2 + 1)
                    nc.scalar.activation(kexp[i][:, c, :], KB[c // 2][:, (c % 2) * TOKENS:(c % 2 + 1) * TOKENS],
                                         ACT.Exp, bias=nkmax[i][:, c:c + 1],
                                         accum_out=ksum[i][:, c:c + 1]).then_inc(kexp_ready[i], 1)

            def q_exp(l, i, t):
                act.wait_ge(qsub_ready[i], TILES * l + t + 1)
                nc.scalar.activation(q[i][:, t, :], q[i][:, t, :], ACT.Exp).then_inc(qexp_ready[i], 1)

            def v_to_sbuf(l, i, t):
                act.wait_ge(v_done[i], TILES * l + t + 1)
                nc.scalar.activation(vtok[i][:, t, :], VB[t][:], ACT.Copy).then_inc(vtok_ready[i], 1)

            def k_to_sbuf(l, i, t):
                act.wait_ge(k_turned[i], TILES * l + t + 1)
                nc.scalar.activation(ktok[i][:, t, :], KB[t][:], ACT.Copy).then_inc(ktok_odd_ready[i], 1)

            def context_blocks(l, i):
                act.wait_ge(ctx_done[i], l + 1)
                act.wait_ge(zeroed, 1)
                for a in range(2):
                    src = VB[0][a * DH:(a + 1) * DH, :].rearrange("p (c d) -> p c d", c=PAIRS)
                    nc.scalar.activation(ctxbd[i][a * DH:(a + 1) * DH, :, a * DH:(a + 1) * DH],
                                         src[:, :, a * DH:(a + 1) * DH], ACT.Copy).then_inc(ctxbd_ready[i], 1)

            def q_to_sbuf(l, i, t):
                act.wait_ge(q_turned[i], TILES * l + t + 1)
                nc.scalar.activation(qT[i][:, t, :], QB[t][:], ACT.Copy).then_inc(qT_ready[i], 1)

            def gelu(l, i):
                for c in range(FC):
                    act.wait_ge(ff1_done[i], 2 * l + c // 2 + 1)
                    src = (SB_ if c < 2 else CB)
                    nc.scalar.activation(hid[i][:, c, :], src[:, (c % 2) * TOKENS:(c % 2 + 1) * TOKENS], ACT.Gelu,
                                         bias=col("ff1_b", l * FC + c)).then_inc(hid_ready[i], 1)

            def phi3_exp(i, t):
                act.wait_ge(qk3m_ready, TILES * i + t + 1)
                nc.scalar.activation(qk3e[i][:, t, :], qk3m[i][:, t, :], ACT.Exp).then_inc(qk3e_ready, 1)

            def v3_to_sbuf(i):
                for t in range(TILES):
                    act.wait_ge(v3_done, TILES * i + t + 1)
                    nc.scalar.activation(v3[i][:, t, :], VB[t][:, 0:E], ACT.Copy).then_inc(v3_ready, 1)

            def context3_to_sbuf(i):
                act.wait_ge(cw3_done, i + 1)
                nc.scalar.activation(cw3[i][:].rearrange("p c e -> p (c e)"), VB[0][0:EC, 0:ECH * E],
                                     ACT.Copy).then_inc(cw3_ready, 1)

            def gelu3(i, first, last):
                act.wait_ge(mixed_weights, 1)
                for hc in range(first, last):
                    act.wait_ge(fc_done, HC // 2 * i + hc // 2 + 1)
                    src = (SB_, CB, SB_)[hc // 2]
                    nc.scalar.activation(hid3[i][:, hc, :], src[:, (hc % 2) * TOKENS:(hc % 2 + 1) * TOKENS],
                                         ACT.Gelu_apprx_tanh, bias=fcb[:, hc:hc + 1]).then_inc(hid3_ready, 1)

            act.wait_ge(loaded["small"], 16)
            embedding_bias(0, KB[0])
            copy_masks()
            act.wait_ge(loaded["qkv0"], 16)
            for third in (1, 0, 2):
                at = slice(third * INNER, (third + 1) * INNER)
                weight_high_part("qkv0", qkvw[0][:, at], qkvw_parts[0][0][:, at])
            embedding_bias(1, QB[0])
            for s in range(STEPS):
                l, i = divmod(s, IMAGES)
                lp, ip = divmod(s - 1, IMAGES)
                k_exp(l, i)
                q_exp(l, i, 0)
                for t in range(TILES):
                    v_to_sbuf(l, i, t)
                q_exp(l, i, 1)
                k_to_sbuf(l, i, 1)
                if s:
                    gelu(lp, ip)
                context_blocks(l, i)
                for t in range(TILES):
                    q_to_sbuf(l, i, t)
                if s < LAYERS:
                    act.wait_ge(loaded[f"rest{s}"], 16)
                    weight_high_part(f"ff1_{s}", ff1w_all(s), ff1w_parts[s][0][:])
                if s == 0:
                    act.wait_ge(loaded["qkv1"], 16)
                    for third in (1, 0, 2):
                        at = slice(third * INNER, (third + 1) * INNER)
                        weight_high_part("qkv1", qkvw[1][:, at], qkvw_parts[1][0][:, at])
                if s == 2:
                    act.wait_ge(loaded["aqkv"], 16)
                    weight_high_part("aqkv", aqkvw, aqkvw_parts[0][:])
                    act.wait_ge(fc_mixed, 1)
                    for c in range(ECH):
                        weight_high_part("fc", fcw[:, c, :], fcw_parts[0][:, c, :])
            gelu(1, 1)
            for t in range(TILES):
                phi3_exp(0, t)
            v3_to_sbuf(0)
            context3_to_sbuf(0)
            for t in range(TILES):
                phi3_exp(1, t)
            v3_to_sbuf(1)
            context3_to_sbuf(1)
            gelu3(0, 0, 4)
            gelu3(0, 4, HC)
            gelu3(1, 0, HC)

        @block.gpsimd
        def _(pool):
            def rsqrt(i, n):
                pool.wait_ge(var_ready[i], n + 1)
                nc.gpsimd.tensor_tensor(rstd[i][:], var[i][:], minus_half[:], ALU.pow).then_inc(rstd_ready[i], 1)

            def add_bias(i, name, l, ready, count):
                pool.wait_ge(loaded["rows"], 16)
                pool.wait_ge(ready, count)
                at = ROW[name] + l * D
                nc.gpsimd.tensor_tensor(xb[i][:], x[i][:], rows_sb[:, at:at + D].unsqueeze(1).to_broadcast([P, TILES, D]),
                                        ALU.add).then_inc(xb_ready[i], 1)

            def normalise_q(l, i, t):
                pool.wait_ge(rqsum_ready[i], TILES * l + t + 1)
                nc.gpsimd.tensor_tensor(qn[i][:, t, :].rearrange("p (h d) -> p h d", h=HEADS),
                                        q[i][:, t, :].rearrange("p (h d) -> p h d", h=HEADS),
                                        rqsum[i][:, t, :].unsqueeze(2).to_broadcast([P, HEADS, DH]),
                                        ALU.mult).then_inc(qn_ready[i], 1)

            def add_bias3(i, which, row, ready):
                pool.wait_ge(ready, 1)
                nc.gpsimd.tensor_tensor(hb[i][:], h[i][:], row.unsqueeze(1).to_broadcast([P, TILES, E]),
                                        ALU.add).then_inc(hb_ready[i], 1)

            def mix_biases():
                pool.wait_ge(mix_copied, 3)
                pool.wait_ge(loaded["rows"], 16)
                b_fc = small_sb[:, P + EC + COL["b_fc"][0]:P + EC + COL["b_fc"][0] + HC]
                nc.gpsimd.tensor_tensor(fcb[:], proj_mix[:, :, ESEG], b_fc, ALU.mult)
                nc.gpsimd.tensor_tensor(projb[:], projb[:], rows_sb[:, ROW["b_proj"]:ROW["b_proj"] + E],
                                        ALU.mult).then_inc(mixed_weights, 1)

            def mix_fc():
                pool.wait_ge(loaded["fc"], 16)
                for c in range(ECH):
                    view = fcw[:, c, :].rearrange("p (s n) -> p s n", n=SEG)
                    last = nc.gpsimd.tensor_tensor(view, view, fc_mix[:, c, :].unsqueeze(2).to_broadcast([EC, HSEG, SEG]),
                                                   ALU.mult)
                last.then_inc(fc_mixed, 1)

            def mix_proj():
                pool.wait_ge(loaded["proj"], 16)
                for c in range(HC):
                    view = projw[:, c, :].rearrange("p (s n) -> p s n", n=SEG)
                    last = nc.gpsimd.tensor_tensor(view, view,
                                                   proj_mix[:, c, 0:ESEG].unsqueeze(2).to_broadcast([P, ESEG, SEG]),
                                                   ALU.mult)
                last.then_inc(mixed_weights, 1)

            def weight_low_part(name, n, raw, hi, lo):
                pool.wait_ge(split_hi[name], n)
                nc.gpsimd.tensor_tensor(lo, raw, hi.bitcast(F32), ALU.subtract).then_inc(split_lo[name], 1)

            pool.wait_ge(loaded["small"], 16)
            pool.wait_ge(consts_set, 2)
            rsqrt(0, LN1(0))
            def third(w, n):
                at = (1, 0, 2)[n] * INNER
                return w[:, at:at + INNER]

            def qkv1_low_part(n):
                weight_low_part("qkv1", n + 1, third(qkvw[1], n), third(qkvw_parts[1][0], n), third(qkvw_parts[1][1], n))

            for s in range(STEPS):
                l, i = divmod(s, IMAGES)
                lp, ip = divmod(s - 1, IMAGES)
                if s:
                    rsqrt(ip, LN2(lp))
                    add_bias(ip, "ff2_b", lp, x_mid[ip], lp + 1)
                if s == 1:
                    for n in range(2):
                        qkv1_low_part(n)
                if s == 2:
                    weight_low_part("ff1_1", 1, ff1w_all(1), ff1w_parts[1][0][:], ff1w_parts[1][1][:])
                if s == 3:
                    weight_low_part("aqkv", 1, aqkvw, aqkvw_parts[0][:], aqkvw_parts[1][:])
                for t in range(TILES):
                    normalise_q(l, i, t)
                if l == 0:
                    add_bias(i, "out_b", 0, x_ready[i], 1)
                else:
                    add_bias(i, "out_b", l, x_new[i], l)
                if s == 1:
                    qkv1_low_part(2)
                if s == 2:
                    mix_fc()
                if s == 3:
                    weight_low_part("fc", 1, fcw[:, 0, :], fcw_parts[0][:, 0, :], fcw_parts[1][:, 0, :])
                rsqrt(1 - i, LN1((s + 1) // 2))
                if s == 0:
                    weight_low_part("ff1_0", 1, ff1w_all(0), ff1w_parts[0][0][:], ff1w_parts[0][1][:])
                    mix_biases()
            rsqrt(1, LN2(1))
            rsqrt(0, LN3)
            add_bias(1, "ff2_b", 1, x_mid[1], LAYERS)
            weight_low_part("fc", 2, fcw[:, 1, :], fcw_parts[0][:, 1, :], fcw_parts[1][:, 1, :])
            rsqrt(1, LNF)
            add_bias3(0, "b_out", rows_sb[:, ROW["b_out"]:ROW["b_out"] + E], h_ready[0])
            mix_proj()
            rsqrt(1, LN3)
            rsqrt(0, LN4)
            add_bias3(0, "b_proj", projb[:], h2_ready[0])
            add_bias3(1, "b_out", rows_sb[:, ROW["b_out"]:ROW["b_out"] + E], h_ready[1])
            rsqrt(1, LN4)
            add_bias3(1, "b_proj", projb[:], h2_ready[1])


def _chunks(w, rows):
    return np.ascontiguousarray(w.reshape(w.shape[0] // rows, rows, w.shape[1]).transpose(1, 0, 2))


def kernel(**inputs):
    import concourse.bacc as bacc
    from concourse.bass_utils import run_bass_kernel_spmd

    a = {k: np.asarray(v) for k, v in inputs.items()}
    T = "L0_tok_"
    g = SIDE // PATCH
    xt = a["x"].reshape(IMAGES, CHANNELS, g, PATCH, g, PATCH).transpose(0, 1, 3, 5, 2, 4)
    xt = xt.reshape(IMAGES, KCONV * P, TOKENS)
    convT = a[T + "conv_w"].reshape(D, KCONV * P).T
    embed0 = _chunks(np.concatenate([convT, xt[0]], axis=1), P)
    patches1 = _chunks(xt[1], P)
    cols = [a[T + "conv_b"][None]]
    cols += [a[T + n] for n in ("ln1_g", "ln1_b", "ln2_g", "ln2_b")]
    cols += [a[T + "ff1_b"].reshape(LAYERS * FC, P), a[T + "lnf_g"][None], a[T + "lnf_b"][None],
             a["L0_ffn_b_fc"].reshape(HC, P)]
    headmask = np.zeros((P, EC), np.float32)
    headmask[:EC] = np.kron(np.eye(EC // D3, dtype=np.float32), np.ones((D3, D3), np.float32))
    small = np.concatenate([np.eye(P, dtype=np.float32), headmask, np.concatenate(cols).T], axis=1)
    rows = np.concatenate([a[T + "out_b"].reshape(-1), a[T + "ff2_b"].reshape(-1), a[T + "head_b"],
                           a["L0_attn_b_out"], a["L0_ffn_b_proj"]])[None]
    rest = [np.concatenate([_chunks(a[T + "out_w"][l], P).reshape(P, -1), a[T + "ff1_w"][l],
                            _chunks(a[T + "ff2_w"][l], P).reshape(P, -1)], axis=1) for l in range(LAYERS)]
    mask_h = np.array([[u < r * e for u in range(HMAX)] for e in EMBED for r in RATIO], np.float32)
    mask_e = np.array([[u < e for u in range(E)] for e in EMBED for r in RATIO], np.float32)
    alpha_e = np.repeat(a["L0_ffn_alpha_e"], len(RATIO))[:, None]
    alpha_r = np.tile(a["L0_ffn_alpha_r"], len(EMBED))[:, None]
    host = {
        "small": small, "embed0": embed0, "patches1": patches1,
        "qkv_w": a[T + "qkv_w"], "rest_w": np.stack(rest), "rows": rows,
        "mix": np.concatenate([mask_h, mask_e, mask_h[:, ::SEG], mask_e[:, ::SEG], alpha_e, alpha_r], axis=1),
        "fc_w": _chunks(a["L0_ffn_w_fc"].T, EC), "proj_w": _chunks(a["L0_ffn_w_proj"].T, P),
        "head_w": a[T + "head_w"], "aqkv_w": _chunks(a["L0_attn_W_qkv"], EC),
        "aout_w": _chunks(a["L0_attn_W_out"], EC),
    }
    host = {k: np.ascontiguousarray(v) for k, v in host.items()}
    nc = bacc.Bacc("TRN2", target_bir_lowering=False, num_devices=1)
    args = {k: nc.dram_tensor(f"in_{k}", v.shape, F32, kind="ExternalInput").ap() for k, v in host.items()}
    out = nc.dram_tensor("out_tokens", (IMAGES, P, TILES, E), F32, kind="ExternalOutput").ap()
    build(nc, out=out, **args)
    r = run_bass_kernel_spmd(nc, [{f"in_{k}": v for k, v in host.items()}], core_ids=[0])
    got = r.results[0]["out_tokens"]
    return np.ascontiguousarray(got.transpose(0, 2, 1, 3)).reshape(IMAGES, TOKENS, E)
```

```python
from contextlib import ExitStack

import numpy as np
import concourse.bass as bass
from concourse import mybir

F32 = mybir.dt.float32
F32R = mybir.dt.float32r
ALU = mybir.AluOpType
ACT = mybir.ActivationFunctionType
AX_X = mybir.AxisListType.X

P = 128
IMAGES, LAYERS = 2, 2
CHANNELS, SIDE, PATCH = 32, 128, 8
TOKENS = (SIDE // PATCH) ** 2
TILES = TOKENS // P
D = 128
KCONV = CHANNELS * PATCH * PATCH // P
HEADS, DH = 8, 64
INNER = HEADS * DH
PAIRS = INNER // P
FF = 512
FC = FF // P
E = 192
EC = 96
ECH = E // EC
H3, D3 = 12, 16
HMAX = 768
HC = HMAX // P
EMBED, RATIO = (96, 144, 192), (2, 3, 4)
MIX = len(EMBED) * len(RATIO)
SEG = 48
HSEG, ESEG = HMAX // SEG, E // SEG
EPS_LN, EPS_Z = 1e-5, 1e-6
STEPS = IMAGES * LAYERS

COL = {}
for _name, _n in (("conv_b", 1), ("ln1_g", LAYERS), ("ln1_b", LAYERS), ("ln2_g", LAYERS), ("ln2_b", LAYERS),
                  ("ff1_b", LAYERS * FC), ("lnf_g", 1), ("lnf_b", 1), ("b_fc", HC)):
    COL[_name] = (sum(n for _, n in COL.values()), _n)
NCOL = sum(n for _, n in COL.values())
ROW, _at = {}, 0
for _name, _n in (("out_b", LAYERS * D), ("ff2_b", LAYERS * D), ("head_b", E), ("b_out", E), ("b_proj", E)):
    ROW[_name] = _at
    _at += _n
NROW = _at
CONV_AT = (0, 1, 4, 8, 12, KCONV)
CONV_PIECES = len(CONV_AT) - 1


def build(nc, small, embed0, patches1, qkv_w, rest_w, rows, mix, fc_w, proj_w, head_w, aqkv_w, aout_w, out):
    with ExitStack() as ctx:
        def sb(name, shape, dt=F32):
            return ctx.enter_context(nc.sbuf_tensor(name, shape, dt))

        def sem(name):
            return ctx.enter_context(nc.semaphore(name))

        def sems(name):
            return [sem(f"{name}{i}") for i in range(IMAGES)]

        def per_image(name, shape):
            return [sb(f"{name}{i}", shape) for i in range(IMAGES)]

        def shared(name, shape):
            return [sb(name, shape)] * IMAGES

        small_sb = sb("small_sb", [P, P + EC + NCOL])
        ident = small_sb[:, 0:P]
        headmask = small_sb[0:EC, P:P + EC]

        def col(name, n=0, parts=P):
            at = P + EC + COL[name][0] + n
            return small_sb[0:parts, at:at + 1]

        embed_sb = sb("embed_sb", [P, KCONV, D + TOKENS])
        patches1_sb = sb("patches1_sb", [P, KCONV, TOKENS])
        spare = embed_sb[:].rearrange("p c n -> p (c n)")
        qkvw = [sb("qkvw0", [P, 3 * INNER]), spare[:, 0:3 * INNER]]
        aqkvw = spare[0:EC, 3 * INNER:3 * INNER + ECH * 3 * E].rearrange("p (c n) -> p c n", c=ECH)
        fc_at = 3 * INNER + ECH * 3 * E
        fcw_raw = spare[0:EC, fc_at:fc_at + ECH * HMAX].rearrange("p (c n) -> p c n", c=ECH)

        def parts(name, shape):
            return sb(f"{name}_hi", shape, F32R), sb(f"{name}_lo", shape, F32R)

        qkvw_parts = [parts(f"qkvw{l}", [P, 3 * INNER]) for l in range(LAYERS)]
        ff1w_parts = [parts(f"ff1w{l}", [P, FF]) for l in range(LAYERS)]
        aqkvw_parts = parts("aqkvw", [EC, ECH, 3 * E])
        fcw_parts = parts("fcw", [EC, ECH, HMAX])
        restw = [sb(f"restw{l}", [P, PAIRS * D + FF + FC * D]) for l in range(LAYERS)]
        rows_sb = sb("rows_sb", [P, NROW])
        mix_sb = sb("mix_sb", [MIX, HMAX + E + HSEG + ESEG + 2])
        mix_at = np.cumsum([0, HMAX, E, HSEG, ESEG, 1, 1])
        mask_h, mask_e, mask_hseg, mask_eseg, alpha_e, alpha_r = (
            mix_sb[:, int(a):int(b)] for a, b in zip(mix_at[:-1], mix_at[1:]))
        projw_raw = sb("projw_raw", [P, HC, E])
        headw = sb("headw", [P, E])
        aoutw = sb("aoutw", [EC, ECH, E])
        ones = sb("ones", [P, E])
        minus_half = sb("minus_half", [P, TILES])
        alpha = sb("alpha", [MIX, P])
        alpha_mask_e = sb("alpha_mask_e", [MIX, E])
        alpha_eseg = sb("alpha_eseg", [MIX, ESEG + 1])
        fc_mix = sb("fc_mix", [EC, ECH, HSEG])
        proj_mix = sb("proj_mix", [P, HC, ESEG + 1])
        fcw = fcw_raw
        projw = projw_raw
        fcb = sb("fcb", [P, HC])
        projb = sb("projb", [P, E])

        def outw(l, p):
            return restw[l][:, p * D:(p + 1) * D]

        def ff1w_all(l):
            return restw[l][:, PAIRS * D:PAIRS * D + FF]

        def ff2w(l, c):
            at = PAIRS * D + FF + c * D
            return restw[l][:, at:at + D]

        embT = per_image("embT", [P, TOKENS])
        x = per_image("x", [P, TILES, D])
        xb = per_image("xb", [P, TILES, D])
        h = per_image("h", [P, TILES, E])
        hb = per_image("hb", [P, TILES, E])
        stats = per_image("stats", [P, TILES, 6])
        mv = per_image("mv", [P, TILES, 2])
        var = per_image("var", [P, TILES])
        rstd = per_image("rstd", [P, TILES])
        xn = per_image("xn", [P, TILES, E])
        yT = per_image("yT", [P, TOKENS])
        yT_hi, yT_lo = (list(z) for z in zip(*(parts(f"yT{i}", [P, TOKENS]) for i in range(IMAGES))))
        yT3_hi, yT3_lo = (list(z) for z in zip(*(parts(f"yT3_{i}", [EC, ECH, TOKENS]) for i in range(IMAGES))))
        nkmax = per_image("nkmax", [P, PAIRS])
        kexp = shared("kexp", [P, PAIRS, TOKENS])
        ksum = per_image("ksum", [P, PAIRS])
        rksum = per_image("rksum", [P, PAIRS])
        ktok = shared("ktok", [P, TILES, INNER])
        vtok = shared("vtok", [P, TILES, INNER])
        nqmax = per_image("nqmax", [P, TILES, HEADS])
        q = shared("q", [P, TILES, INNER])
        qsum = per_image("qsum", [P, TILES, HEADS])
        rqsum = per_image("rqsum", [P, TILES, HEADS])
        qn = shared("qn", [P, TILES, INNER])
        qT = shared("qT", [P, TILES, INNER])
        ctxbd = shared("ctxbd", [P, PAIRS, P])
        cw = shared("cw", [P, PAIRS, D])
        hid = shared("hid", [P, FC, TOKENS])
        qk3m = [b[:, :, 0:2 * E] for b in q]
        qk3e = [b[:].rearrange("p c t -> p (c t)").rearrange("p (t n) -> p t n", t=TILES)[:, :, 0:2 * E] for b in kexp]
        qk3 = [b[:, :, 0:2 * E] for b in ktok]
        v3 = [b[:, :, 0:E] for b in vtok]
        qks3 = [b[:, :, 0:E] for b in qT]
        qz3 = [b[:, :, 0:E] for b in qn]
        hid3 = [patches1_sb[:, HC * i:HC * (i + 1), :] for i in range(IMAGES)]
        kv3 = per_image("kv3", [EC, ECH, EC])
        den3 = per_image("den3", [P, TILES, H3])
        z3 = per_image("z3", [P, TILES, H3])
        qzT3 = per_image("qzT3", [EC, ECH, TOKENS])
        cw3 = per_image("cw3", [EC, ECH, E])
        outs = per_image("outs", [P, TILES, E])

        bank = [ctx.enter_context(nc.psum_tensor(f"bank{i}", [P, 512], F32)) for i in range(8)]
        KB, QB, VB = bank[0:2], bank[2:4], bank[4:6]
        SB_, CB = bank[6], bank[7]
        FF2, FF2_LAST = KB, VB
        HB = [KB[0], SB_]
        T3, T4 = [KB[1], KB[0]], [SB_, CB]
        FB = [[SB_, CB, KB[0]], [KB[0], KB[1], SB_]]

        loaded = {n: sem(f"loaded_{n}") for n in (
            ["small", "mix", "rows", "fc", "proj", "head", "aqkv", "aout", "patches1a", "patches1b", "qkv0_k"]
            + [f"embed{j}" for j in range(CONV_PIECES)]
            + [f"qkv{l}" for l in range(LAYERS)] + [f"rest{l}" for l in range(LAYERS)])}
        consts_set = sem("consts_set")
        alpha_ready = sem("alpha_ready")
        mix_psum = sem("mix_psum")
        mix_copied = sem("mix_copied")
        split_hi, split_lo = ({n: sem(f"{n}_{part}") for n in ("qkv0", "qkv1", "ff1_0", "ff1_1", "aqkv", "fc")}
                              for part in ("hi", "lo"))
        fc_mixed = sem("fc_mixed")
        mixed_weights = sem("mixed_weights")
        conv_done = sem("conv_done")
        embT_ready, emb_turned, x_ready = (sems(n) for n in ("embT_ready", "emb_turned", "x_ready"))
        stats_done, mv_done, var_ready, rstd_ready, xn_ready, turned, yT_ready, yT_hi_ready, yT_lo_ready = (
            sems(n) for n in ("stats_done", "mv_done", "var_ready", "rstd_ready", "xn_ready", "turned", "yT_ready",
                              "yT_hi_ready", "yT_lo_ready"))
        xb_ready, k_done, nkmax_ready, kexp_ready, k_turned, ktok_ready, ktok_odd_ready = (
            sems(n) for n in ("xb_ready", "k_done", "nkmax_ready", "kexp_ready", "k_turned", "ktok_ready",
                              "ktok_odd_ready"))
        yT3_hi0_ready = sem("yT3_hi0_ready")
        v_done, vtok_ready, q_done, nqmax_ready, qsub_ready, qexp_ready, qsum_ready, rqsum_ready, qn_ready = (
            sems(n) for n in ("v_done", "vtok_ready", "q_done", "nqmax_ready", "qsub_ready", "qexp_ready",
                              "qsum_ready", "rqsum_ready", "qn_ready"))
        q_turned, qT_even_ready, qT_odd_ready, ctx_done, ctxbd_ready, cw_done, rksum_ready, cw_ready, att_done = (
            sems(n) for n in ("q_turned", "qT_even_ready", "qT_odd_ready", "ctx_done", "ctxbd_ready", "cw_done", "rksum_ready",
                              "cw_ready", "att_done"))
        x_mid, ff1_done, hid_ready, ff2_done, x_new = (
            sems(n) for n in ("x_mid", "ff1_done", "hid_ready", "ff2_done", "x_new"))
        h_ready, hb_ready, h2_ready, outs_ready = (
            sems(n) for n in ("h_ready", "hb_ready", "h2_ready", "outs_ready"))
        stored = sem("stored")
        head_done, qk3_done, v3_done, qk3m_ready, qk3e_ready, qk3_ready, v3_ready = (
            sem(n) for n in ("head_done", "qk3_done", "v3_done", "qk3m_ready", "qk3e_ready", "qk3_ready", "v3_ready"))
        kv3_done, kv3_ready, qks3_ready, den3_sum, den3_ready, z3_ready, qz3_ready = (
            sem(n) for n in ("kv3_done", "kv3_ready", "qks3_ready", "den3_sum", "den3_ready",
                             "z3_ready", "qz3_ready"))
        ksum3_done = sem("ksum3_done")
        cw3_done, cw3_ready, qz3_turned, qzT3_ready, out3_done, fc_done, hid3_ready, proj_done = (
            sem(n) for n in ("cw3_done", "cw3_ready", "qz3_turned", "qzT3_ready", "out3_done", "fc_done",
                             "hid3_ready", "proj_done"))

        def LN1(l):
            return 2 * l

        def LN2(l):
            return 2 * l + 1

        LNF, LN3, LN4 = 2 * LAYERS, 2 * LAYERS + 1, 2 * LAYERS + 2

        block = ctx.enter_context(nc.Block())

        @block.sync
        def _(sp):
            half = KCONV // 2
            for j in range(CONV_PIECES):
                at = slice(CONV_AT[j], CONV_AT[j + 1])
                sp.dma_start(embed_sb[:, at, :], embed0[:, at, :]).then_inc(loaded[f"embed{j}"], 16)
                if j == 1:
                    sp.dma_start(mix_sb[:], mix).then_inc(loaded["mix"], 16)
                    sp.dma_start(small_sb[:], small).then_inc(loaded["small"], 16)
            sp.dma_start(patches1_sb[:, 0:half, :], patches1[:, 0:half, :]).then_inc(loaded["patches1a"], 16)
            k_columns = slice(INNER, 2 * INNER)
            sp.dma_start(qkvw[0][:, k_columns], qkv_w[0][:, k_columns]).then_inc(loaded["qkv0_k"], 16)
            for at in (slice(0, INNER), slice(2 * INNER, 3 * INNER)):
                sp.dma_start(qkvw[0][:, at], qkv_w[0][:, at]).then_inc(loaded["qkv0"], 16)
            sp.dma_start(patches1_sb[:, half:, :], patches1[:, half:, :]).then_inc(loaded["patches1b"], 16)
            sp.dma_start(restw[0][:], rest_w[0]).then_inc(loaded["rest0"], 16)
            sp.dma_start(rows_sb[:], rows.to_broadcast([P, NROW])).then_inc(loaded["rows"], 16)
            sp.dma_start(projw_raw[:], proj_w).then_inc(loaded["proj"], 16)
            sp.dma_start(restw[1][:], rest_w[1]).then_inc(loaded["rest1"], 16)
            sp.dma_start(headw[:], head_w).then_inc(loaded["head"], 16)
            sp.dma_start(aoutw[:], aout_w).then_inc(loaded["aout"], 16)
            sp.wait_ge(conv_done, IMAGES)
            sp.dma_start(qkvw[1], qkv_w[1]).then_inc(loaded["qkv1"], 16)
            sp.dma_start(aqkvw, aqkv_w).then_inc(loaded["aqkv"], 16)
            sp.dma_start(fcw_raw, fc_w).then_inc(loaded["fc"], 16)
            for i in range(IMAGES):
                for t in range(TILES):
                    sp.wait_ge(outs_ready[i], t + 1)
                    sp.dma_start(out[i, :, t, :], outs[i][:, t, :]).then_inc(stored, 16)
            sp.wait_ge(stored, 16 * TILES * IMAGES)

        @block.tensor
        def _(pe):
            def split_product(order, dst, left, right, low_ready, chunks, stages):
                for k, (a, b) in enumerate(order):
                    last = k == len(order) - 1
                    if ("low" if last else "high") not in stages:
                        continue
                    if last:
                        pe.wait_ge(*low_ready)
                    for n in range(chunks):
                        mm = nc.tensor.matmul(dst, left(a, n), right(b, n), start=(k == 0 and n == 0),
                                              stop=(last and n == chunks - 1))
                return mm

            def weight_left(dst, left, right, low_ready, chunks=1, stages=("high", "low")):
                return split_product([(0, 0), (1, 0), (0, 1)], dst, left, right, low_ready, chunks, stages)

            def weight_right(dst, left, right, low_ready, chunks=1, stages=("high", "low")):
                return split_product([(0, 0), (0, 1), (1, 0)], dst, left, right, low_ready, chunks, stages)

            def conv(i, dst, first=0, last=KCONV):
                for c in range(first, last):
                    if i == 0 and c in CONV_AT:
                        pe.wait_ge(loaded[f"embed{CONV_AT.index(c)}"], 16)
                    if i == 1 and c % (KCONV // 2) == 0:
                        pe.wait_ge(loaded["patches1a" if c == 0 else "patches1b"], 16)
                    rhs = embed_sb[:, c, D:] if i == 0 else patches1_sb[:, c, :]
                    mm = nc.tensor.matmul(dst[:, 0:TOKENS], embed_sb[:, c, 0:D], rhs,
                                          start=(c == 0), stop=(c == KCONV - 1))
                if last == KCONV:
                    mm.then_inc(conv_done, 1)

            def embedding_to_tokens(i, dst):
                pe.wait_ge(embT_ready[i], 1)
                for t in range(TILES):
                    mm = nc.tensor.transpose(dst[:, t * D:(t + 1) * D], embT[i][:, t * P:(t + 1) * P], ident)
                mm.then_inc(emb_turned[i], 1)

            def turn_norm(i, n, dst):
                pe.wait_ge(xn_ready[i], n + 1)
                for t in range(TILES):
                    if n <= LNF:
                        mm = nc.tensor.transpose(dst[:, t * P:(t + 1) * P], xn[i][:, t, 0:D], ident)
                    else:
                        for c in range(ECH):
                            mm = nc.tensor.transpose(dst[c][0:EC, t * P:(t + 1) * P], xn[i][:, t, c * EC:(c + 1) * EC], ident)
                mm.then_inc(turned[i], 1)

            def qkv_k(l, i):
                pe.wait_ge(split_lo[f"qkv{l}"], 1)
                pe.wait_ge(yT_hi_ready[i], LN1(l) + 1)
                for b in range(2):
                    for c in range(2):
                        at = INNER + (2 * b + c) * P
                        mm = weight_left(KB[b][:, c * TOKENS:(c + 1) * TOKENS],
                                         lambda part, n: qkvw_parts[l][part][:, at:at + P],
                                         lambda part, n: (yT_hi, yT_lo)[part][i][:],
                                         (yT_lo_ready[i], LN1(l) + 1))
                    mm.then_inc(k_done[i], 1)

            def qkv_q(l, i, stage):
                if stage == "high":
                    pe.wait_ge(split_lo[f"qkv{l}"], 2)
                    pe.wait_ge(yT_hi_ready[i], LN1(l) + 1)
                for t in range(TILES):
                    mm = weight_right(QB[t][:], lambda part, n: (yT_hi, yT_lo)[part][i][:, t * P:(t + 1) * P],
                                      lambda part, n: qkvw_parts[l][part][:, 0:INNER],
                                      (yT_lo_ready[i], LN1(l) + 1), stages=(stage,))
                    if stage == "low":
                        mm.then_inc(q_done[i], 1)

            def qkv_v(l, i, t):
                if t == 0:
                    pe.wait_ge(split_lo[f"qkv{l}"], 3)
                    if l or i:
                        pe.wait_ge(x_mid[1 - i], l + i)
                weight_right(VB[t][:], lambda part, n: (yT_hi, yT_lo)[part][i][:, t * P:(t + 1) * P],
                             lambda part, n: qkvw_parts[l][part][:, 2 * INNER:3 * INNER],
                             (yT_lo_ready[i], LN1(l) + 1)).then_inc(v_done[i], 1)

            def turn_k(l, i):
                pe.wait_ge(kexp_ready[i], PAIRS * (l + 1))
                for t in range(TILES):
                    for c in range(PAIRS):
                        mm = nc.tensor.transpose(KB[t][:, c * P:(c + 1) * P], kexp[i][:, c, t * P:(t + 1) * P], ident)
                    mm.then_inc(k_turned[i], 1)

            def context(l, i):
                pe.wait_ge(vtok_ready[i], TILES * (l + 1))
                pe.wait_ge(ktok_ready[i], l + 1)
                pe.wait_ge(ktok_odd_ready[i], l + 1)
                for p in range(PAIRS):
                    for t in range(TILES):
                        mm = nc.tensor.matmul(VB[0][:, p * P:(p + 1) * P], vtok[i][:, t, p * P:(p + 1) * P],
                                              ktok[i][:, t, p * P:(p + 1) * P], start=(t == 0), stop=(t == TILES - 1))
                mm.then_inc(ctx_done[i], 1)

            def context_out(l, i):
                pe.wait_ge(loaded[f"rest{l}"], 16)
                pe.wait_ge(ctxbd_ready[i], 2 * (l + 1))
                for p in range(PAIRS):
                    mm = nc.tensor.matmul(VB[1][:, p * D:(p + 1) * D], ctxbd[i][:, p, :], outw(l, p),
                                          start=True, stop=True)
                mm.then_inc(cw_done[i], 1)

            def turn_q(l, i, t):
                pe.wait_ge(qn_ready[i], TILES * l + t + 1)
                for c in range(PAIRS):
                    mm = nc.tensor.transpose(QB[t][:, c * P:(c + 1) * P], qn[i][:, t, c * P:(c + 1) * P], ident)
                mm.then_inc(q_turned[i], 1)

            def attend(l, i, t, first, last):
                pe.wait_ge((qT_even_ready, qT_odd_ready)[t][i], l + 1)
                for c in range(first, last):
                    if t == 0:
                        pe.wait_ge(cw_ready[i], PAIRS * l + c + 1)
                    mm = nc.tensor.matmul(VB[0][:, t * D:(t + 1) * D], qT[i][:, t, c * P:(c + 1) * P],
                                          cw[i][:, c, :], start=(c == 0), stop=(c == PAIRS - 1))
                if t == TILES - 1 and last == PAIRS:
                    mm.then_inc(att_done[i], 1)

            def ff1(l, i):
                pe.wait_ge(split_lo[f"ff1_{l}"], 1)
                pe.wait_ge(yT_hi_ready[i], LN2(l) + 1)
                for c, stages in ((2, ("high",)), (0, ("high",)), (0, ("low",)), (1, ("high", "low")),
                                  (2, ("low",)), (3, ("high", "low"))):
                    if c == 0 and stages == ("high",):
                        pe.wait_ge(yT_ready[i], LN2(l) + 1)
                    dst = (SB_ if c < 2 else CB)
                    mm = weight_left(dst[:, (c % 2) * TOKENS:(c % 2 + 1) * TOKENS],
                                     lambda part, n: ff1w_parts[l][part][:, c * P:(c + 1) * P],
                                     lambda part, n: (yT_hi, yT_lo)[part][i][:],
                                     (yT_lo_ready[i], LN2(l) + 1), stages=stages)
                    if c % 2:
                        mm.then_inc(ff1_done[i], 1)

            def ff2(l, i, banks):
                for c in range(FC):
                    pe.wait_ge(hid_ready[i], FC * l + c + 1)
                    for t in range(TILES):
                        mm = nc.tensor.matmul(banks[t][:, 0:D], hid[i][:, c, t * P:(t + 1) * P],
                                              ff2w(l, c), start=(c == 0), stop=(c == FC - 1))
                mm.then_inc(ff2_done[i], 1)

            def mix_fc_masks():
                pe.wait_ge(loaded["mix"], 16)
                pe.wait_ge(alpha_ready, 3)
                for c in range(ECH):
                    nc.tensor.matmul(SB_[0:EC, c * HSEG:(c + 1) * HSEG], alpha_mask_e[:, c * EC:(c + 1) * EC],
                                     mask_hseg, start=True, stop=True)
                nc.tensor.matmul(SB_[:, 128:128 + E], alpha[:], mask_e, start=True, stop=True).then_inc(mix_psum, 1)

            def mix_proj_masks():
                for c in range(HC):
                    at = c * (ESEG + 1)
                    mm = nc.tensor.matmul(KB[1][:, at:at + ESEG + 1], mask_h[:, c * P:(c + 1) * P], alpha_eseg[:],
                                          start=True, stop=True)
                mm.then_inc(mix_psum, 1)

            def head(i):
                pe.wait_ge(loaded["head"], 16)
                pe.wait_ge(yT_ready[i], LNF + 1)
                for t in range(TILES):
                    mm = nc.tensor.matmul(HB[i][:, t * E:(t + 1) * E], yT[i][:, t * P:(t + 1) * P], headw[:],
                                          start=True, stop=True)
                mm.then_inc(head_done, 1)

            def qkv3(i):
                pe.wait_ge(split_lo["aqkv"], ECH)
                pe.wait_ge(yT_hi_ready[i], LN3)
                pe.wait_ge(yT3_hi0_ready, i + 1)
                for stage in ("high", "low"):
                    for t in range(TILES):
                        mm = weight_right(QB[t][:, 0:2 * E],
                                          lambda part, c: (yT3_hi, yT3_lo)[part][i][:, c, t * P:(t + 1) * P],
                                          lambda part, c: aqkvw_parts[part][:, c, 0:2 * E],
                                          (yT_lo_ready[i], LN3), ECH, stages=(stage,))
                        if stage == "low":
                            mm.then_inc(qk3_done, 1)
                if i == 0:
                    pe.wait_ge(x_new[1], LAYERS)
                if i == 0:
                    pe.wait_ge(x_mid[1], LAYERS)
                else:
                    pe.wait_ge(h2_ready[0], 1)
                for t in range(TILES):
                    weight_right(VB[t][:, 0:E],
                                 lambda part, c: (yT3_hi, yT3_lo)[part][i][:, c, t * P:(t + 1) * P],
                                 lambda part, c: aqkvw_parts[part][:, c, 2 * E:3 * E],
                                 (yT_lo_ready[i], LN3), ECH).then_inc(v3_done, 1)

            def k3_over_tokens(i):
                pe.wait_ge(qk3_ready, TILES * i + TILES)
                for t in range(TILES):
                    nc.tensor.matmul(KB[1][:, 0:E], ones[:, 0:P], qk3[i][:, t, E:2 * E],
                                     start=(t == 0), stop=False)
                nc.tensor.matmul(KB[1][:, 0:E], ones[0:1, 0:P], ones[0:1, 0:E],
                                 start=False, stop=True).then_inc(ksum3_done, 1)

            def context3(i):
                pe.wait_ge(v3_ready, TILES * i + TILES)
                for c in range(ECH):
                    for t in range(TILES):
                        mm = nc.tensor.matmul(KB[0][0:EC, c * EC:(c + 1) * EC], v3[i][:, t, c * EC:(c + 1) * EC],
                                              qk3[i][:, t, E + c * EC:E + (c + 1) * EC],
                                              start=(t == 0), stop=(t == TILES - 1))
                mm.then_inc(kv3_done, 1)

            def context_out3(i):
                pe.wait_ge(loaded["aout"], 16)
                pe.wait_ge(kv3_ready, i + 1)
                for c in range(ECH):
                    mm = nc.tensor.matmul(VB[0][0:EC, c * E:(c + 1) * E], kv3[i][:, c, :], aoutw[:, c, :],
                                          start=True, stop=True)
                mm.then_inc(cw3_done, 1)

            def turn_q3(i):
                pe.wait_ge(qz3_ready, i + 1)
                for t in range(TILES):
                    for c in range(ECH):
                        at = c * TOKENS + t * P
                        mm = nc.tensor.transpose(QB[0][0:EC, at:at + P], qz3[i][:, t, c * EC:(c + 1) * EC], ident)
                mm.then_inc(qz3_turned, 1)

            def attend3(i, t):
                if t == 0:
                    pe.wait_ge(cw3_ready, i + 1)
                    pe.wait_ge(qzT3_ready, i + 1)
                for c in range(ECH):
                    mm = nc.tensor.matmul(VB[1][:, t * E:(t + 1) * E], qzT3[i][:, c, t * P:(t + 1) * P],
                                          cw3[i][:, c, :], start=(c == 0), stop=(c == ECH - 1))
                if t == TILES - 1:
                    mm.then_inc(out3_done, 1)

            def fc3(i, g):
                if g == 0:
                    pe.wait_ge(split_lo["fc"], ECH)
                    pe.wait_ge(yT_hi_ready[i], LN4)
                    pe.wait_ge(yT3_hi0_ready, IMAGES + i + 1)
                if g == 0 and i == 0:
                    pe.wait_ge(yT_lo_ready[i], LN4)
                dst = FB[i][g]
                for j in range(2):
                    hc = 2 * g + j
                    mm = weight_left(dst[:, j * TOKENS:(j + 1) * TOKENS],
                                     lambda part, c: fcw_parts[part][:, c, hc * P:(hc + 1) * P],
                                     lambda part, c: (yT3_hi, yT3_lo)[part][i][:, c, :],
                                     (yT_lo_ready[i], LN4), ECH)
                mm.then_inc(fc_done, 1)

            def proj3(i, first, last):
                pe.wait_ge(mixed_weights, 2)
                if i and first == 0:
                    pe.wait_ge(outs_ready[0], TILES)
                for c in range(first, last):
                    pe.wait_ge(hid3_ready, HC * i + c + 1)
                    for t in range(TILES):
                        mm = nc.tensor.matmul(QB[t][:, 0:E], hid3[i][:, c, t * P:(t + 1) * P],
                                              projw[:, c, :], start=(c == 0), stop=(c == HC - 1))
                        if c == HC - 1:
                            mm.then_inc(proj_done, 1)

            conv(0, KB[0], 0, CONV_AT[2])
            mix_fc_masks()
            conv(0, KB[0], CONV_AT[2], KCONV)
            pe.wait_ge(loaded["small"], 16)
            embedding_to_tokens(0, KB[1])
            pe.wait_ge(mix_copied, 2)
            conv(1, SB_, 0, 6)
            turn_norm(0, LN1(0), CB)
            conv(1, SB_, 6, 8)
            for s in range(STEPS):
                l, i = divmod(s, IMAGES)
                lp, ip = divmod(s - 1, IMAGES)
                qkv_q(l, i, "high")
                qkv_k(l, i)
                qkv_q(l, i, "low")
                qkv_v(l, i, 0)
                if s:
                    turn_norm(ip, LN2(lp), SB_)
                qkv_v(l, i, 1)
                turn_k(l, i)
                if s == 0:
                    conv(1, SB_, 8, 12)
                if s:
                    ff1(lp, ip)
                context(l, i)
                if s == 0:
                    conv(1, SB_, 12, KCONV)
                turn_q(l, i, 0)
                if s:
                    ff2(lp, ip, FF2)
                if s == 0:
                    embedding_to_tokens(1, CB)
                context_out(l, i)
                turn_q(l, i, 1)
                attend(l, i, 0, 0, PAIRS)
                attend(l, i, 1, 0, PAIRS // 2)
                turn_norm(1 - i, LN1((s + 1) // 2), CB)
                attend(l, i, 1, PAIRS // 2, PAIRS)
            head(0)
            mix_proj_masks()
            turn_norm(1, LN2(1), QB[0])
            ff1(1, 1)
            turn_norm(0, LN3, T3)
            ff2(1, 1, FF2_LAST)
            qkv3(0)
            turn_norm(1, LNF, CB)
            k3_over_tokens(0)
            head(1)
            context3(0)
            turn_q3(0)
            context_out3(0)
            attend3(0, 0)
            turn_norm(1, LN3, T3)
            attend3(0, 1)
            qkv3(1)
            turn_norm(0, LN4, T4)
            k3_over_tokens(1)
            context3(1)
            fc3(0, 0)
            context_out3(1)
            turn_q3(1)
            fc3(0, 1)
            for t in range(TILES):
                attend3(1, t)
            fc3(0, 2)
            proj3(0, 0, 4)
            turn_norm(1, LN4, T4)
            proj3(0, 4, HC)
            for g in range(3):
                fc3(1, g)
            proj3(1, 0, HC)

        @block.vector
        def _(dve):
            def norm_stats(i, n, src, width, ready, count):
                dve.wait_ge(ready, count)
                for t in range(TILES):
                    nc.vector.bn_stats(stats[i][:, t, :], src[:, t, 0:width]).then_inc(stats_done[i], 1)
                for t in range(TILES):
                    dve.wait_ge(stats_done[i], TILES * n + t + 1)
                    nc.vector.bn_aggr(mv[i][:, t, :], stats[i][:, t, :]).then_inc(mv_done[i], 1)
                dve.wait_ge(mv_done[i], TILES * (n + 1))
                nc.vector.tensor_scalar(var[i][:], mv[i][:, :, 1], EPS_LN, None, ALU.add).then_inc(var_ready[i], 1)

            def norm_apply(i, n, src, width):
                dve.wait_ge(rstd_ready[i], n + 1)
                for t in range(TILES):
                    last = nc.vector.tensor_scalar(xn[i][:, t, 0:width], src[:, t, 0:width], mv[i][:, t, 0:1],
                                                   rstd[i][:, t:t + 1], ALU.subtract, ALU.mult)
                last.then_inc(xn_ready[i], 1)

            def norm_out_hi(i, n, bankof, g, b):
                dve.wait_ge(turned[i], n + 1)
                nc.vector.tensor_scalar(yT_hi[i][:], bankof[:, 0:TOKENS], g, b, ALU.mult,
                                        ALU.add).then_inc(yT_hi_ready[i], 1)

            def norm_out_lo(i, n):
                dve.wait_ge(yT_ready[i], n + 1)
                dve.wait_ge(yT_hi_ready[i], n + 1)
                nc.vector.tensor_tensor(yT_lo[i][:], yT[i][:], yT_hi[i][:].bitcast(F32),
                                        ALU.subtract).then_inc(yT_lo_ready[i], 1)

            def norm_out3(i, n, banks):
                dve.wait_ge(turned[i], n + 1)
                nc.vector.tensor_copy(yT3_hi[i][:, 0, :], banks[0][0:EC, 0:TOKENS]).then_inc(yT3_hi0_ready, 1)
                dve.wait_ge(yT3_hi0_ready, IMAGES * (n - LN3) + i + 1)
                nc.vector.tensor_tensor(yT3_lo[i][:, 0, :], banks[0][0:EC, 0:TOKENS], yT3_hi[i][:, 0, :].bitcast(F32),
                                        ALU.subtract)
                dve.wait_ge(yT_hi_ready[i], n)
                nc.vector.tensor_tensor(yT3_lo[i][:, 1, :], banks[1][0:EC, 0:TOKENS], yT3_hi[i][:, 1, :].bitcast(F32),
                                        ALU.subtract).then_inc(yT_lo_ready[i], 1)

            def weight_low_part(name, n, raw, hi, lo):
                dve.wait_ge(split_hi[name], n)
                nc.vector.tensor_tensor(lo, raw, hi.bitcast(F32), ALU.subtract).then_inc(split_lo[name], 1)

            def x_from_embedding(i, bankof):
                dve.wait_ge(emb_turned[i], 1)
                nc.vector.tensor_copy(x[i][:].rearrange("p t d -> p (t d)"),
                                      bankof[:, 0:TILES * D]).then_inc(x_ready[i], 1)

            def k_max(l, i):
                for b in range(2):
                    dve.wait_ge(k_done[i], 2 * l + b + 1)
                    nc.vector.tensor_reduce(nkmax[i][:, 2 * b:2 * b + 2],
                                            KB[b][:].rearrange("p (c t) -> p c t", c=2), AX_X, ALU.max,
                                            negate=True).then_inc(nkmax_ready[i], 1)

            def q_max(l, i, t):
                dve.wait_ge(q_done[i], TILES * l + t + 1)
                nc.vector.tensor_reduce(nqmax[i][:, t, :], QB[t][:].rearrange("p (h d) -> p h d", h=HEADS),
                                        AX_X, ALU.max, negate=True).then_inc(nqmax_ready[i], 1)

            def q_shift(l, i, t):
                dve.wait_ge(nqmax_ready[i], TILES * l + t + 1)
                nc.vector.tensor_tensor(q[i][:, t, :].rearrange("p (h d) -> p h d", h=HEADS),
                                        QB[t][:].rearrange("p (h d) -> p h d", h=HEADS),
                                        nqmax[i][:, t, :].unsqueeze(2).to_broadcast([P, HEADS, DH]),
                                        ALU.add).then_inc(qsub_ready[i], 1)

            def q_sum(l, i, t):
                dve.wait_ge(qexp_ready[i], TILES * l + t + 1)
                nc.vector.tensor_reduce(qsum[i][:, t, :], q[i][:, t, :].rearrange("p (h d) -> p h d", h=HEADS),
                                        AX_X, ALU.add).then_inc(qsum_ready[i], 1)

            def q_inverse_sum(l, i, t):
                dve.wait_ge(qsum_ready[i], TILES * l + t + 1)
                nc.vector.reciprocal(rqsum[i][:, t, :], qsum[i][:, t, :]).then_inc(rqsum_ready[i], 1)

            def k_to_sbuf(l, i, t):
                dve.wait_ge(k_turned[i], TILES * l + 1)
                nc.vector.tensor_copy(ktok[i][:, t, :], KB[t][:]).then_inc(ktok_ready[i], 1)

            def k_inverse_sum(l, i):
                dve.wait_ge(kexp_ready[i], PAIRS * (l + 1))
                nc.vector.reciprocal(rksum[i][:], ksum[i][:]).then_inc(rksum_ready[i], 1)

            def context_blocks(l, i):
                dve.wait_ge(ctx_done[i], l + 1)
                dve.wait_ge(consts_set, 3)
                for a in range(2):
                    src = VB[0][a * DH:(a + 1) * DH, :].rearrange("p (c d) -> p c d", c=PAIRS)
                    nc.vector.tensor_scalar(ctxbd[i][a * DH:(a + 1) * DH, :, a * DH:(a + 1) * DH],
                                            src[:, :, a * DH:(a + 1) * DH], DH ** -0.5, None,
                                            ALU.mult).then_inc(ctxbd_ready[i], 1)

            def q_to_sbuf(l, i, t):
                dve.wait_ge(q_turned[i], TILES * l + t + 1)
                nc.vector.tensor_copy(qT[i][:, t, :], QB[t][:]).then_inc(qT_even_ready[i], 1)

            def add_attention(l, i):
                dve.wait_ge(att_done[i], l + 1)
                dve.wait_ge(xb_ready[i], 2 * l + 1)
                nc.vector.tensor_tensor(x[i][:].rearrange("p t d -> p (t d)"), VB[0][:, 0:TILES * D],
                                        xb[i][:].rearrange("p t d -> p (t d)"), ALU.add).then_inc(x_mid[i], 1)

            def add_ff(l, i, banks):
                dve.wait_ge(ff2_done[i], l + 1)
                dve.wait_ge(xb_ready[i], 2 * l + 2)
                for t in range(TILES):
                    last = nc.vector.tensor_tensor(x[i][:, t, :], banks[t][:, 0:D], xb[i][:, t, :], ALU.add)
                last.then_inc(x_new[i], 1)

            def bias_row(name):
                return rows_sb[:, ROW[name]:ROW[name] + E].unsqueeze(1).to_broadcast([P, TILES, E])

            def h_from_head(i):
                dve.wait_ge(head_done, i + 1)
                dve.wait_ge(loaded["rows"], 16)
                nc.vector.tensor_tensor(h[i][:], HB[i][:, 0:TILES * E].rearrange("p (t e) -> p t e", t=TILES),
                                        bias_row("head_b"), ALU.add).then_inc(h_ready[i], 1)

            def phi3_min(i, t):
                dve.wait_ge(qk3_done, TILES * i + t + 1)
                nc.vector.tensor_scalar(qk3m[i][:, t, :], QB[t][:, 0:2 * E], 0.0, None,
                                        ALU.min).then_inc(qk3m_ready, 1)

            def phi3_sum(i, t):
                dve.wait_ge(qk3e_ready, TILES * i + t + 1)
                nc.vector.scalar_tensor_tensor(out=qk3[i][:, t, :], in0=QB[t][:, 0:2 * E], scalar=0.0,
                                               in1=qk3e[i][:, t, :], op0=ALU.max, op1=ALU.add).then_inc(qk3_ready, 1)

            def q3_times_k_sum(i):
                dve.wait_ge(ksum3_done, i + 1)
                nc.vector.tensor_tensor(qks3[i], qk3[i][:, :, 0:E],
                                        KB[1][:, 0:E].unsqueeze(1).to_broadcast([P, TILES, E]),
                                        ALU.mult).then_inc(qks3_ready, 1)

            def k3_denominator(i):
                dve.wait_ge(qks3_ready, i + 1)
                nc.vector.tensor_reduce(den3[i][:],
                                        qks3[i].rearrange("p t (h d) -> p t h d", d=D3),
                                        AX_X, ALU.add).then_inc(den3_sum, 1)

            def z3_from_denominator(i):
                dve.wait_ge(den3_sum, i + 1)
                nc.vector.tensor_scalar(den3[i][:], den3[i][:], EPS_Z, None, ALU.add).then_inc(den3_ready, 1)
                dve.wait_ge(den3_ready, i + 1)
                nc.vector.reciprocal(z3[i][:], den3[i][:]).then_inc(z3_ready, 1)

            def z3_apply(i):
                dve.wait_ge(z3_ready, i + 1)
                nc.vector.tensor_tensor(qz3[i].rearrange("p t (h d) -> p t h d", d=D3), qk3_q(i),
                                        z3[i][:].unsqueeze(3).to_broadcast([P, TILES, H3, D3]), ALU.mult).then_inc(qz3_ready, 1)

            def qk3_q(i):
                return qk3[i][:, :, 0:E].rearrange("p t (h d) -> p t h d", d=D3)

            def kv3_masked(i):
                dve.wait_ge(kv3_done, i + 1)
                nc.vector.tensor_tensor(kv3[i][:], KB[0][0:EC, 0:ECH * EC].rearrange("p (c e) -> p c e", c=ECH),
                                        headmask.unsqueeze(1).to_broadcast([EC, ECH, EC]),
                                        ALU.mult).then_inc(kv3_ready, 1)

            def q3_to_sbuf(i):
                dve.wait_ge(qz3_turned, i + 1)
                nc.vector.tensor_copy(qzT3[i][:].rearrange("p c t -> p (c t)"),
                                      QB[0][0:EC, 0:ECH * TOKENS]).then_inc(qzT3_ready, 1)

            def add_attention3(i):
                dve.wait_ge(out3_done, i + 1)
                dve.wait_ge(hb_ready[i], 1)
                nc.vector.tensor_tensor(h[i][:].rearrange("p t e -> p (t e)"), VB[1][:, 0:TILES * E],
                                        hb[i][:].rearrange("p t e -> p (t e)"), ALU.add).then_inc(h2_ready[i], 1)

            def add_ff3(i):
                dve.wait_ge(hb_ready[i], 2)
                for t in range(TILES):
                    dve.wait_ge(proj_done, TILES * i + t + 1)
                    nc.vector.tensor_tensor(outs[i][:, t, :], QB[t][:, 0:E], hb[i][:, t, :],
                                            ALU.add).then_inc(outs_ready[i], 1)

            nc.vector.memset(ones[:], 1.0).then_inc(consts_set, 1)
            nc.vector.memset(minus_half[:], -0.5).then_inc(consts_set, 1)
            nc.vector.memset(ctxbd[0][:], 0.0).then_inc(consts_set, 1)
            dve.wait_ge(loaded["mix"], 16)
            dve.wait_ge(consts_set, 1)
            nc.vector.tensor_scalar(alpha[:], ones[0:MIX, 0:P], alpha_e, alpha_r, ALU.mult, ALU.mult).then_inc(alpha_ready, 1)
            nc.vector.tensor_scalar(alpha_mask_e[:], mask_e, alpha_e, alpha_r, ALU.mult, ALU.mult).then_inc(alpha_ready, 1)
            nc.vector.tensor_scalar(alpha_eseg[:, 0:ESEG], mask_eseg, alpha_e, alpha_r, ALU.mult, ALU.mult)
            nc.vector.tensor_scalar(alpha_eseg[:, ESEG:], ones[0:MIX, 0:1], alpha_e, alpha_r,
                                    ALU.mult, ALU.mult).then_inc(alpha_ready, 1)
            x_from_embedding(0, KB[1])
            norm_stats(0, LN1(0), x[0], D, x_ready[0], 1)
            def qkv0_low_part(n):
                at = slice((1, 0, 2)[n] * INNER, ((1, 0, 2)[n] + 1) * INNER)
                weight_low_part("qkv0", n + 1, qkvw[0][:, at], qkvw_parts[0][0][:, at], qkvw_parts[0][1][:, at])

            qkv0_low_part(0)
            norm_apply(0, LN1(0), x[0], D)
            qkv0_low_part(1)
            norm_out_hi(0, LN1(0), CB, col("ln1_g", 0), col("ln1_b", 0))
            qkv0_low_part(2)
            norm_out_lo(0, LN1(0))
            for s in range(STEPS):
                l, i = divmod(s, IMAGES)
                lp, ip = divmod(s - 1, IMAGES)
                if s:
                    norm_stats(ip, LN2(lp), x[ip], D, x_mid[ip], lp + 1)
                k_max(l, i)
                if s:
                    norm_apply(ip, LN2(lp), x[ip], D)
                q_max(l, i, 0)
                if s:
                    norm_out_hi(ip, LN2(lp), SB_, col("ln2_g", lp), col("ln2_b", lp))
                q_shift(l, i, 0)
                q_max(l, i, 1)
                q_shift(l, i, 1)
                k_to_sbuf(l, i, 0)
                q_sum(l, i, 0)
                q_inverse_sum(l, i, 0)
                q_sum(l, i, 1)
                k_inverse_sum(l, i)
                q_inverse_sum(l, i, 1)
                context_blocks(l, i)
                q_to_sbuf(l, i, 0)
                if s:
                    add_ff(lp, ip, FF2)
                    norm_stats(ip, LN1(lp + 1), x[ip], D, x_new[ip], lp + 1)
                else:
                    x_from_embedding(1, CB)
                    norm_stats(1, LN1(0), x[1], D, x_ready[1], 1)
                norm_apply(1 - i, LN1((s + 1) // 2), x[1 - i], D)
                if s < STEPS - 1:
                    ln = (s + 1) // 2
                    norm_out_hi(1 - i, LN1(ln), CB, col("ln1_g", ln), col("ln1_b", ln))
                    add_attention(l, i)
                    norm_out_lo(1 - i, LN1(ln))
            add_attention(1, 1)
            norm_stats(1, LN2(1), x[1], D, x_mid[1], LAYERS)
            h_from_head(0)
            norm_apply(1, LN2(1), x[1], D)
            norm_out_hi(1, LN2(1), QB[0], col("ln2_g", 1), col("ln2_b", 1))
            norm_stats(0, LN3, h[0], E, h_ready[0], 1)
            norm_out_lo(1, LN2(1))
            norm_apply(0, LN3, h[0], E)
            norm_out3(0, LN3, T3)
            add_ff(1, 1, FF2_LAST)
            norm_stats(1, LNF, x[1], D, x_new[1], LAYERS)
            for t in range(TILES):
                phi3_min(0, t)
            norm_apply(1, LNF, x[1], D)
            for t in range(TILES):
                phi3_sum(0, t)
            q3_times_k_sum(0)
            k3_denominator(0)
            h_from_head(1)
            z3_from_denominator(0)
            z3_apply(0)
            kv3_masked(0)
            norm_stats(1, LN3, h[1], E, h_ready[1], 1)
            norm_apply(1, LN3, h[1], E)
            norm_out3(1, LN3, T3)
            add_attention3(0)
            norm_stats(0, LN4, h[0], E, h2_ready[0], 1)
            for t in range(TILES):
                phi3_min(1, t)
            norm_apply(0, LN4, h[0], E)
            for t in range(TILES):
                phi3_sum(1, t)
            norm_out3(0, LN4, T4)
            q3_times_k_sum(1)
            k3_denominator(1)
            kv3_masked(1)
            z3_from_denominator(1)
            z3_apply(1)
            q3_to_sbuf(1)
            add_attention3(1)
            norm_stats(1, LN4, h[1], E, h2_ready[1], 1)
            norm_apply(1, LN4, h[1], E)
            norm_out3(1, LN4, T4)
            add_ff3(0)
            add_ff3(1)

        @block.scalar
        def _(act):
            def embedding_bias(i, bankof):
                act.wait_ge(conv_done, i + 1)
                nc.scalar.activation(embT[i][:], bankof[:, 0:TOKENS], ACT.Identity,
                                     bias=col("conv_b")).then_inc(embT_ready[i], 1)

            def copy_fc_masks():
                act.wait_ge(mix_psum, 1)
                nc.scalar.activation(fc_mix[:].rearrange("p c s -> p (c s)"), SB_[0:EC, 0:ECH * HSEG],
                                     ACT.Copy).then_inc(mix_copied, 1)
                nc.scalar.activation(projb[:], SB_[:, 128:128 + E], ACT.Copy).then_inc(mix_copied, 1)

            def copy_proj_masks():
                act.wait_ge(mix_psum, 2)
                nc.scalar.activation(proj_mix[:].rearrange("p c s -> p (c s)"), KB[1][:, 0:HC * (ESEG + 1)],
                                     ACT.Copy).then_inc(mix_copied, 1)

            def norm_out(i, n, bankof, g, b):
                act.wait_ge(turned[i], n + 1)
                if n != LNF:
                    act.wait_ge(yT_hi_ready[i], n + 1)
                nc.scalar.activation(yT[i][:], bankof[:, 0:TOKENS], ACT.Identity, bias=b,
                                     scale=g).then_inc(yT_ready[i], 1)

            def norm_out3_hi1(i, n, banks):
                act.wait_ge(turned[i], n + 1)
                nc.scalar.activation(yT3_hi[i][:, 1, :], banks[1][0:EC, 0:TOKENS],
                                     ACT.Copy).then_inc(yT_hi_ready[i], 1)

            def q3_to_sbuf(i):
                act.wait_ge(qz3_turned, i + 1)
                nc.scalar.activation(qzT3[i][:].rearrange("p c t -> p (c t)"),
                                     QB[0][0:EC, 0:ECH * TOKENS], ACT.Copy).then_inc(qzT3_ready, 1)

            def weight_high_part(name, raw, hi):
                nc.scalar.activation(hi, raw, ACT.Copy).then_inc(split_hi[name], 1)

            def k_exp(l, i):
                for c in range(PAIRS):
                    act.wait_ge(nkmax_ready[i], 2 * l + c // 2 + 1)
                    nc.scalar.activation(kexp[i][:, c, :], KB[c // 2][:, (c % 2) * TOKENS:(c % 2 + 1) * TOKENS],
                                         ACT.Exp, bias=nkmax[i][:, c:c + 1],
                                         accum_out=ksum[i][:, c:c + 1]).then_inc(kexp_ready[i], 1)

            def q_exp(l, i, t):
                act.wait_ge(qsub_ready[i], TILES * l + t + 1)
                nc.scalar.activation(q[i][:, t, :], q[i][:, t, :], ACT.Exp).then_inc(qexp_ready[i], 1)

            def v_to_sbuf(l, i, t):
                act.wait_ge(v_done[i], TILES * l + t + 1)
                nc.scalar.activation(vtok[i][:, t, :], VB[t][:], ACT.Copy).then_inc(vtok_ready[i], 1)

            def k_to_sbuf(l, i, t):
                act.wait_ge(k_turned[i], TILES * l + t + 1)
                nc.scalar.activation(ktok[i][:, t, :], KB[t][:], ACT.Copy).then_inc(ktok_odd_ready[i], 1)

            def context_scaled(l, i):
                act.wait_ge(cw_done[i], l + 1)
                act.wait_ge(rksum_ready[i], l + 1)
                for c in range(PAIRS):
                    nc.scalar.activation(cw[i][:, c, :], VB[1][:, c * D:(c + 1) * D], ACT.Copy,
                                         scale=rksum[i][:, c:c + 1]).then_inc(cw_ready[i], 1)

            def q_to_sbuf(l, i, t):
                act.wait_ge(q_turned[i], TILES * l + t + 1)
                nc.scalar.activation(qT[i][:, t, :], QB[t][:], ACT.Copy).then_inc(qT_odd_ready[i], 1)

            def gelu(l, i):
                for c in range(FC):
                    act.wait_ge(ff1_done[i], 2 * l + c // 2 + 1)
                    src = (SB_ if c < 2 else CB)
                    nc.scalar.activation(hid[i][:, c, :], src[:, (c % 2) * TOKENS:(c % 2 + 1) * TOKENS], ACT.Gelu,
                                         bias=col("ff1_b", l * FC + c)).then_inc(hid_ready[i], 1)

            def phi3_exp(i, t):
                act.wait_ge(qk3m_ready, TILES * i + t + 1)
                nc.scalar.activation(qk3e[i][:, t, :], qk3m[i][:, t, :], ACT.Exp).then_inc(qk3e_ready, 1)

            def v3_to_sbuf(i):
                for t in range(TILES):
                    act.wait_ge(v3_done, TILES * i + t + 1)
                    nc.scalar.activation(v3[i][:, t, :], VB[t][:, 0:E], ACT.Copy).then_inc(v3_ready, 1)

            def context3_to_sbuf(i):
                act.wait_ge(cw3_done, i + 1)
                nc.scalar.activation(cw3[i][:].rearrange("p c e -> p (c e)"), VB[0][0:EC, 0:ECH * E],
                                     ACT.Copy).then_inc(cw3_ready, 1)

            def gelu3(i, first, last):
                act.wait_ge(mixed_weights, 1)
                for hc in range(first, last):
                    act.wait_ge(fc_done, HC // 2 * i + hc // 2 + 1)
                    src = FB[i][hc // 2]
                    nc.scalar.activation(hid3[i][:, hc, :], src[:, (hc % 2) * TOKENS:(hc % 2 + 1) * TOKENS],
                                         ACT.Gelu_apprx_tanh, bias=fcb[:, hc:hc + 1]).then_inc(hid3_ready, 1)

            copy_fc_masks()
            act.wait_ge(loaded["small"], 16)
            embedding_bias(0, KB[0])
            act.wait_ge(loaded["qkv0_k"], 16)
            for third in (1, 0, 2):
                if third == 0:
                    act.wait_ge(loaded["qkv0"], 32)
                at = slice(third * INNER, (third + 1) * INNER)
                weight_high_part("qkv0", qkvw[0][:, at], qkvw_parts[0][0][:, at])
            norm_out(0, LN1(0), CB, col("ln1_g", 0), col("ln1_b", 0))
            for s in range(STEPS):
                l, i = divmod(s, IMAGES)
                lp, ip = divmod(s - 1, IMAGES)
                k_exp(l, i)
                if s:
                    norm_out(ip, LN2(lp), SB_, col("ln2_g", lp), col("ln2_b", lp))
                q_exp(l, i, 0)
                for t in range(TILES):
                    v_to_sbuf(l, i, t)
                k_to_sbuf(l, i, 1)
                q_exp(l, i, 1)
                if s == 0:
                    embedding_bias(1, SB_)
                if s:
                    gelu(lp, ip)
                if s < LAYERS:
                    act.wait_ge(loaded[f"rest{s}"], 16)
                    weight_high_part(f"ff1_{s}", ff1w_all(s), ff1w_parts[s][0][:])
                if s == 2:
                    act.wait_ge(loaded["aqkv"], 16)
                    weight_high_part("aqkv", aqkvw, aqkvw_parts[0][:])
                if s == 3:
                    for c in range(ECH):
                        act.wait_ge(fc_mixed, c + 1)
                        weight_high_part("fc", fcw[:, c, :], fcw_parts[0][:, c, :])
                context_scaled(l, i)
                q_to_sbuf(l, i, 1)
                ln = (s + 1) // 2
                g, b = (col("lnf_g"), col("lnf_b")) if s == STEPS - 1 else (col("ln1_g", ln), col("ln1_b", ln))
                norm_out(1 - i, LN1(ln), CB, g, b)
                if s == 0:
                    act.wait_ge(loaded["qkv1"], 16)
                    for third in (1, 0, 2):
                        at = slice(third * INNER, (third + 1) * INNER)
                        weight_high_part("qkv1", qkvw[1][:, at], qkvw_parts[1][0][:, at])
            copy_proj_masks()
            norm_out(1, LN2(1), QB[0], col("ln2_g", 1), col("ln2_b", 1))
            gelu(1, 1)
            norm_out3_hi1(0, LN3, T3)
            for t in range(TILES):
                phi3_exp(0, t)
            norm_out(1, LNF, CB, col("lnf_g"), col("lnf_b"))
            v3_to_sbuf(0)
            q3_to_sbuf(0)
            context3_to_sbuf(0)
            norm_out3_hi1(1, LN3, T3)
            for t in range(TILES):
                phi3_exp(1, t)
            v3_to_sbuf(1)
            norm_out3_hi1(0, LN4, T4)
            context3_to_sbuf(1)
            gelu3(0, 0, HC)
            norm_out3_hi1(1, LN4, T4)
            gelu3(1, 0, HC)

        @block.gpsimd
        def _(pool):
            def rsqrt(i, n):
                pool.wait_ge(var_ready[i], n + 1)
                nc.gpsimd.tensor_tensor(rstd[i][:], var[i][:], minus_half[:], ALU.pow).then_inc(rstd_ready[i], 1)

            def norm_out_lo(i, n):
                pool.wait_ge(yT_ready[i], n + 1)
                pool.wait_ge(yT_hi_ready[i], n + 1)
                nc.gpsimd.tensor_tensor(yT_lo[i][:], yT[i][:], yT_hi[i][:].bitcast(F32),
                                        ALU.subtract).then_inc(yT_lo_ready[i], 1)

            def add_bias(i, name, l, ready, count):
                pool.wait_ge(loaded["rows"], 16)
                pool.wait_ge(ready, count)
                at = ROW[name] + l * D
                nc.gpsimd.tensor_tensor(xb[i][:], x[i][:], rows_sb[:, at:at + D].unsqueeze(1).to_broadcast([P, TILES, D]),
                                        ALU.add).then_inc(xb_ready[i], 1)

            def normalise_q(l, i, t):
                pool.wait_ge(rqsum_ready[i], TILES * l + t + 1)
                nc.gpsimd.tensor_tensor(qn[i][:, t, :].rearrange("p (h d) -> p h d", h=HEADS),
                                        q[i][:, t, :].rearrange("p (h d) -> p h d", h=HEADS),
                                        rqsum[i][:, t, :].unsqueeze(2).to_broadcast([P, HEADS, DH]),
                                        ALU.mult).then_inc(qn_ready[i], 1)

            def add_bias3(i, which, row, ready):
                pool.wait_ge(ready, 1)
                nc.gpsimd.tensor_tensor(hb[i][:], h[i][:], row.unsqueeze(1).to_broadcast([P, TILES, E]),
                                        ALU.add).then_inc(hb_ready[i], 1)

            def mix_biases():
                pool.wait_ge(mix_copied, 3)
                pool.wait_ge(loaded["rows"], 16)
                b_fc = small_sb[:, P + EC + COL["b_fc"][0]:P + EC + COL["b_fc"][0] + HC]
                nc.gpsimd.tensor_tensor(fcb[:], proj_mix[:, :, ESEG], b_fc, ALU.mult)
                nc.gpsimd.tensor_tensor(projb[:], projb[:], rows_sb[:, ROW["b_proj"]:ROW["b_proj"] + E],
                                        ALU.mult).then_inc(mixed_weights, 1)

            def mix_fc(c):
                pool.wait_ge(loaded["fc"], 16)
                view = fcw[:, c, :].rearrange("p (s n) -> p s n", n=SEG)
                nc.gpsimd.tensor_tensor(view, view, fc_mix[:, c, :].unsqueeze(2).to_broadcast([EC, HSEG, SEG]),
                                        ALU.mult).then_inc(fc_mixed, 1)

            def mix_proj():
                pool.wait_ge(loaded["proj"], 16)
                for c in range(HC):
                    view = projw[:, c, :].rearrange("p (s n) -> p s n", n=SEG)
                    last = nc.gpsimd.tensor_tensor(view, view,
                                                   proj_mix[:, c, 0:ESEG].unsqueeze(2).to_broadcast([P, ESEG, SEG]),
                                                   ALU.mult)
                last.then_inc(mixed_weights, 1)

            def weight_low_part(name, n, raw, hi, lo):
                pool.wait_ge(split_hi[name], n)
                nc.gpsimd.tensor_tensor(lo, raw, hi.bitcast(F32), ALU.subtract).then_inc(split_lo[name], 1)

            pool.wait_ge(loaded["small"], 16)
            pool.wait_ge(consts_set, 2)
            rsqrt(0, LN1(0))

            def third(w, n):
                at = (1, 0, 2)[n] * INNER
                return w[:, at:at + INNER]

            def qkv1_low_part(n):
                weight_low_part("qkv1", n + 1, third(qkvw[1], n), third(qkvw_parts[1][0], n), third(qkvw_parts[1][1], n))

            for s in range(STEPS):
                l, i = divmod(s, IMAGES)
                lp, ip = divmod(s - 1, IMAGES)
                if s:
                    rsqrt(ip, LN2(lp))
                    add_bias(ip, "ff2_b", lp, x_mid[ip], lp + 1)
                if s == 1:
                    qkv1_low_part(0)
                if s == 2:
                    weight_low_part("ff1_1", 1, ff1w_all(1), ff1w_parts[1][0][:], ff1w_parts[1][1][:])
                if s == 3:
                    weight_low_part("aqkv", 1, aqkvw[:, 0, :], aqkvw_parts[0][:, 0, :], aqkvw_parts[1][:, 0, :])
                if s:
                    norm_out_lo(ip, LN2(lp))
                for t in range(TILES):
                    normalise_q(l, i, t)
                if l == 0:
                    add_bias(i, "out_b", 0, x_ready[i], 1)
                else:
                    add_bias(i, "out_b", l, x_new[i], l)
                if s == 1:
                    qkv1_low_part(1)
                if s == 3:
                    weight_low_part("aqkv", 1, aqkvw[:, 1, :], aqkvw_parts[0][:, 1, :], aqkvw_parts[1][:, 1, :])
                if s == 2:
                    mix_fc(0)
                rsqrt(1 - i, LN1((s + 1) // 2))
                if s == 1:
                    qkv1_low_part(2)
                if s == 2:
                    mix_fc(1)
                if s == 3:
                    weight_low_part("fc", 1, fcw[:, 0, :], fcw_parts[0][:, 0, :], fcw_parts[1][:, 0, :])
                if s == 0:
                    weight_low_part("ff1_0", 1, ff1w_all(0), ff1w_parts[0][0][:], ff1w_parts[0][1][:])
            rsqrt(1, LN2(1))
            rsqrt(0, LN3)
            add_bias(1, "ff2_b", 1, x_mid[1], LAYERS)
            weight_low_part("fc", 2, fcw[:, 1, :], fcw_parts[0][:, 1, :], fcw_parts[1][:, 1, :])
            rsqrt(1, LNF)
            add_bias3(0, "b_out", rows_sb[:, ROW["b_out"]:ROW["b_out"] + E], h_ready[0])
            mix_biases()
            mix_proj()
            rsqrt(1, LN3)
            rsqrt(0, LN4)
            add_bias3(0, "b_proj", projb[:], h2_ready[0])
            add_bias3(1, "b_out", rows_sb[:, ROW["b_out"]:ROW["b_out"] + E], h_ready[1])
            rsqrt(1, LN4)
            add_bias3(1, "b_proj", projb[:], h2_ready[1])


def _chunks(w, rows):
    return np.ascontiguousarray(w.reshape(w.shape[0] // rows, rows, w.shape[1]).transpose(1, 0, 2))


def kernel(**inputs):
    import concourse.bacc as bacc
    from concourse.bass_utils import run_bass_kernel_spmd

    a = {k: np.asarray(v) for k, v in inputs.items()}
    T = "L0_tok_"
    g = SIDE // PATCH
    xt = a["x"].reshape(IMAGES, CHANNELS, g, PATCH, g, PATCH).transpose(0, 1, 3, 5, 2, 4)
    xt = xt.reshape(IMAGES, KCONV * P, TOKENS)
    convT = a[T + "conv_w"].reshape(D, KCONV * P).T
    embed0 = _chunks(np.concatenate([convT, xt[0]], axis=1), P)
    patches1 = _chunks(xt[1], P)
    cols = [a[T + "conv_b"][None]]
    cols += [a[T + n] for n in ("ln1_g", "ln1_b", "ln2_g", "ln2_b")]
    cols += [a[T + "ff1_b"].reshape(LAYERS * FC, P), a[T + "lnf_g"][None], a[T + "lnf_b"][None],
             a["L0_ffn_b_fc"].reshape(HC, P)]
    headmask = np.zeros((P, EC), np.float32)
    headmask[:EC] = np.kron(np.eye(EC // D3, dtype=np.float32), np.ones((D3, D3), np.float32))
    small = np.concatenate([np.eye(P, dtype=np.float32), headmask, np.concatenate(cols).T], axis=1)
    rows = np.concatenate([a[T + "out_b"].reshape(-1), a[T + "ff2_b"].reshape(-1), a[T + "head_b"],
                           a["L0_attn_b_out"], a["L0_ffn_b_proj"]])[None]
    rest = [np.concatenate([_chunks(a[T + "out_w"][l], P).reshape(P, -1), a[T + "ff1_w"][l],
                            _chunks(a[T + "ff2_w"][l], P).reshape(P, -1)], axis=1) for l in range(LAYERS)]
    mask_h = np.array([[u < r * e for u in range(HMAX)] for e in EMBED for r in RATIO], np.float32)
    mask_e = np.array([[u < e for u in range(E)] for e in EMBED for r in RATIO], np.float32)
    alpha_e = np.repeat(a["L0_ffn_alpha_e"], len(RATIO))[:, None]
    alpha_r = np.tile(a["L0_ffn_alpha_r"], len(EMBED))[:, None]
    host = {
        "small": small, "embed0": embed0, "patches1": patches1,
        "qkv_w": a[T + "qkv_w"], "rest_w": np.stack(rest), "rows": rows,
        "mix": np.concatenate([mask_h, mask_e, mask_h[:, ::SEG], mask_e[:, ::SEG], alpha_e, alpha_r], axis=1),
        "fc_w": _chunks(a["L0_ffn_w_fc"].T, EC), "proj_w": _chunks(a["L0_ffn_w_proj"].T, P),
        "head_w": a[T + "head_w"], "aqkv_w": _chunks(a["L0_attn_W_qkv"], EC),
        "aout_w": _chunks(a["L0_attn_W_out"], EC),
    }
    host = {k: np.ascontiguousarray(v) for k, v in host.items()}
    nc = bacc.Bacc("TRN2", target_bir_lowering=False, num_devices=1)
    args = {k: nc.dram_tensor(f"in_{k}", v.shape, F32, kind="ExternalInput").ap() for k, v in host.items()}
    out = nc.dram_tensor("out_tokens", (IMAGES, P, TILES, E), F32, kind="ExternalOutput").ap()
    build(nc, out=out, **args)
    r = run_bass_kernel_spmd(nc, [{f"in_{k}": v for k, v in host.items()}], core_ids=[0])
    got = r.results[0]["out_tokens"]
    return np.ascontiguousarray(got.transpose(0, 2, 1, 3)).reshape(IMAGES, TOKENS, E)
```
